# Optimizing a Trainium2 kernel written in Bass

```python
import numpy as np
import jax
import jax.numpy as jnp

def _softmax(x, axis=-1):
    return jax.nn.softmax(x, axis=axis)

def _gelu(x):
    return jax.nn.gelu(x, approximate=True)

def _silu(x):
    return jax.nn.silu(x)

def _sigmoid(x):
    return jax.nn.sigmoid(x)

def _layernorm(x, axis=-1, eps=1e-05):
    m = jnp.mean(x, axis=axis, keepdims=True)
    v = jnp.var(x, axis=axis, keepdims=True)
    return (x - m) / jnp.sqrt(v + eps)

def _scatter_add(tgt, idx, src, axis=0):
    return tgt.at[idx].add(src)

def _segment_sum(src, seg, n):
    return jax.ops.segment_sum(src, seg, n)
kernel_name = 'mk_xattn_ffn_d1_seqx_r4_373030'

def setup_inputs(seed: int=0):
    np.random.seed(seed)
    _w = jnp.asarray

    def _rec_inputs():
        import jax
        import jax.numpy as jnp
        _rk = jax.random.key(seed)
        x = -0.0002928 + 1 * jax.random.normal(jax.random.fold_in(_rk, 1), (16, 256, 256), jnp.float32)
        _lenS = 256 - jax.random.randint(jax.random.fold_in(_rk, 7), (16,), 0, max(1, 256 // 4) + 1, jnp.int32)
        _lenS2 = 77 - jax.random.randint(jax.random.fold_in(_rk, 8), (16,), 0, max(1, 77 // 4) + 1, jnp.int32)
        _ctx_1024P = jax.random.normal(jax.random.fold_in(_rk, 11), (16, 16, 256), jnp.float32)
        _ctx_1024c = jax.random.dirichlet(jax.random.fold_in(_rk, 511), 0.3 * jnp.ones((16,), jnp.float32), (16, 77))
        _ctx_1024t = jnp.einsum('bsk,bkd->bsd', _ctx_1024c, _ctx_1024P)
        _ctx_1024t = _ctx_1024t * jax.lax.rsqrt(jnp.mean(jnp.square(_ctx_1024t)) + 1e-12) * 0.953939
        ctx_1024 = -1.39393e-06 + 0.999914 * (_ctx_1024t + 0.3 * jax.random.normal(jax.random.fold_in(_rk, 611), (16, 77, 256), jnp.float32))
        return (x, ctx_1024)
    x, ctx_1024 = _rec_inputs()

    def _L0_xattn_setup():
        import jax, jax.numpy as jnp
        import numpy as np
        D_MODEL = 256
        N_HEADS = 16
        HEAD_DIM = D_MODEL // N_HEADS

        def sparsemax(x):
            x = x - jnp.max(x, axis=-1, keepdims=True)
            zs = -jnp.sort(-x, axis=-1)
            L = x.shape[-1]
            rho = jnp.arange(1, L + 1, dtype=x.dtype)
            cssv = jnp.cumsum(zs, axis=-1) - 1.0
            support = zs > cssv / rho
            k = jnp.maximum(jnp.sum(support, axis=-1, keepdims=True), 1)
            tau = jnp.take_along_axis(cssv, k - 1, axis=-1) / k.astype(x.dtype)
            return jnp.clip(x - tau, 0.0)

        def _split_heads(x):
            B, L, _ = x.shape
            return x.reshape(B, L, N_HEADS, HEAD_DIM).transpose(0, 2, 1, 3)
        key = jax.random.key(seed)
        ks = jax.random.split(key, 11)
        B, L = (2, 512)
        s = 0.02
        inp = {'q': jax.random.normal(ks[0], (B, L, D_MODEL), jnp.float32), 'k': jax.random.normal(ks[1], (B, L, D_MODEL), jnp.float32), 'v': jax.random.normal(ks[2], (B, L, D_MODEL), jnp.float32), 'Wq': jax.random.normal(ks[3], (D_MODEL, D_MODEL), jnp.float32) * s, 'bq': jnp.zeros((D_MODEL,), jnp.float32), 'Wk': jax.random.normal(ks[4], (D_MODEL, D_MODEL), jnp.float32) * s, 'bk': jnp.zeros((D_MODEL,), jnp.float32), 'Wv': jax.random.normal(ks[5], (D_MODEL, D_MODEL), jnp.float32) * s, 'bv': jnp.zeros((D_MODEL,), jnp.float32), 'Wo': jax.random.normal(ks[6], (D_MODEL, D_MODEL), jnp.float32) * s, 'bo': jnp.zeros((D_MODEL,), jnp.float32)}
        return inp
    _L0_xattn_all = _L0_xattn_setup()
    _L0_xattn_in = {k: v for k, v in _L0_xattn_all.items() if k in ('Wq', 'bq', 'Wk', 'bk', 'Wv', 'bv', 'Wo', 'bo')}
    del _L0_xattn_all

    def _L0_ffn_setup():
        import jax, jax.numpy as jnp
        import numpy as np
        E = 8
        K = 2
        D = 256
        H = 256
        B, T = (2, 256)
        key = jax.random.key(seed)
        ks = jax.random.split(key, 6)
        s = 0.02
        return {'x': jax.random.normal(ks[0], (B, T, D), dtype=jnp.float32), 'gate_w': jax.random.normal(ks[1], (E, D), dtype=jnp.float32) * s, 'lb_bias': jnp.zeros((E,), dtype=jnp.float32), 'w1': jax.random.normal(ks[2], (E, H, D), dtype=jnp.float32) * s, 'w2': jax.random.normal(ks[3], (E, D, H), dtype=jnp.float32) * s, 'cfc': jax.random.normal(ks[4], (H, D), dtype=jnp.float32) * s, 'cproj': jax.random.normal(ks[5], (D, H), dtype=jnp.float32) * s}
    _L0_ffn_all = _L0_ffn_setup()
    _L0_ffn_in = {k: v for k, v in _L0_ffn_all.items() if k in ('gate_w', 'lb_bias', 'w1', 'w2', 'cfc', 'cproj')}
    del _L0_ffn_all
    return {'x': x, 'ctx_1024': ctx_1024, 'L0_xattn_Wq': _L0_xattn_in['Wq'], 'L0_xattn_bq': _L0_xattn_in['bq'], 'L0_xattn_Wk': _L0_xattn_in['Wk'], 'L0_xattn_bk': _L0_xattn_in['bk'], 'L0_xattn_Wv': _L0_xattn_in['Wv'], 'L0_xattn_bv': _L0_xattn_in['bv'], 'L0_xattn_Wo': _L0_xattn_in['Wo'], 'L0_xattn_bo': _L0_xattn_in['bo'], 'L0_ffn_gate_w': _L0_ffn_in['gate_w'], 'L0_ffn_lb_bias': _L0_ffn_in['lb_bias'], 'L0_ffn_w1': _L0_ffn_in['w1'], 'L0_ffn_w2': _L0_ffn_in['w2'], 'L0_ffn_cfc': _L0_ffn_in['cfc'], 'L0_ffn_cproj': _L0_ffn_in['cproj']}

def reference(x, ctx_1024, L0_xattn_Wq, L0_xattn_bq, L0_xattn_Wk, L0_xattn_bk, L0_xattn_Wv, L0_xattn_bv, L0_xattn_Wo, L0_xattn_bo, L0_ffn_gate_w, L0_ffn_lb_bias, L0_ffn_w1, L0_ffn_w2, L0_ffn_cfc, L0_ffn_cproj):
    import jax
    import jax.numpy as jnp

    def _L0_xattn_ref(q, k, v, Wq, bq, Wk, bk, Wv, bv, Wo, bo):
        import jax, jax.numpy as jnp
        import numpy as np
        D_MODEL = 256
        N_HEADS = 16
        HEAD_DIM = D_MODEL // N_HEADS

        def sparsemax(x):
            x = x - jnp.max(x, axis=-1, keepdims=True)
            zs = -jnp.sort(-x, axis=-1)
            L = x.shape[-1]
            rho = jnp.arange(1, L + 1, dtype=x.dtype)
            cssv = jnp.cumsum(zs, axis=-1) - 1.0
            support = zs > cssv / rho
            k = jnp.maximum(jnp.sum(support, axis=-1, keepdims=True), 1)
            tau = jnp.take_along_axis(cssv, k - 1, axis=-1) / k.astype(x.dtype)
            return jnp.clip(x - tau, 0.0)

        def _split_heads(x):
            B, L, _ = x.shape
            return x.reshape(B, L, N_HEADS, HEAD_DIM).transpose(0, 2, 1, 3)
        qh = _split_heads(q @ Wq + bq)
        kh = _split_heads(k @ Wk + bk)
        vh = _split_heads(v @ Wv + bv)
        scale = HEAD_DIM ** (-0.5)
        scores = jnp.einsum('bhqd,bhkd->bhqk', qh, kh) * scale
        attn = sparsemax(scores)
        out = jnp.einsum('bhqk,bhkd->bhqd', attn, vh)
        B, L = (q.shape[0], q.shape[1])
        out = out.transpose(0, 2, 1, 3).reshape(B, L, D_MODEL)
        return out @ Wo + bo

    def _L0_ffn_ref(x, gate_w, lb_bias, w1, w2, cfc, cproj):
        import jax, jax.numpy as jnp
        import numpy as np
        E = 8
        K = 2
        D = 256
        H = 256
        B, T = (2, 256)
        Bx, Tx, Dx = x.shape
        logits = jnp.einsum('btd,ed->bte', x, gate_w)
        _, idx = jax.lax.top_k(logits + lb_bias, K)
        sel_logits = jnp.take_along_axis(logits, idx, axis=-1)
        w = jax.nn.sigmoid(sel_logits)
        w = w / (jnp.sum(w, axis=-1, keepdims=True) + 1e-06)
        xf = x.reshape(-1, Dx)
        idxf = idx.reshape(-1, K)
        wf = w.reshape(-1, K)
        onehot = jax.nn.one_hot(idxf, E, dtype=wf.dtype)
        we = jnp.einsum('nke,nk->ne', onehot, wf)
        hidden = jnp.square(jax.nn.relu(jnp.einsum('nd,ehd->neh', xf, w1)))
        expert_out = jnp.einsum('neh,edh->ned', hidden, w2)
        moe_out = jnp.einsum('ned,ne->nd', expert_out, we).reshape(Bx, Tx, Dx)
        sh = jnp.square(jax.nn.relu(jnp.einsum('btd,hd->bth', x, cfc)))
        shared = jnp.einsum('bth,dh->btd', sh, cproj)
        return moe_out + shared
    x = x + _L0_xattn_ref(_layernorm(x, axis=-1), ctx_1024, ctx_1024, L0_xattn_Wq, L0_xattn_bq, L0_xattn_Wk, L0_xattn_bk, L0_xattn_Wv, L0_xattn_bv, L0_xattn_Wo, L0_xattn_bo)
    x = x + _L0_ffn_ref(_layernorm(x, axis=-1), L0_ffn_gate_w, L0_ffn_lb_bias, L0_ffn_w1, L0_ffn_w2, L0_ffn_cfc, L0_ffn_cproj)
    return x

_drawn_inputs = setup_inputs


def setup_inputs(seed=0):
    import zlib

    import numpy as np

    out = dict(_drawn_inputs(seed))
    spreads = {'L0_xattn_bq': (0.0, 0.466),
     'L0_xattn_bk': (0.0, 2.0),
     'L0_xattn_bv': (0.0, 0.1),
     'L0_xattn_bo': (0.0, 0.1),
     'L0_ffn_lb_bias': (0.0, 2.0)}
    factors = {'L0_ffn_gate_w': 8.248}
    for name, (base, spread) in spreads.items():
        noise = np.random.default_rng([zlib.crc32(name.encode()), seed]).standard_normal(out[name].shape)
        drawn = base * np.exp(spread * noise) if base else spread * noise
        out[name] = jnp.asarray(drawn.astype(out[name].dtype))
    for name, factor in factors.items():
        out[name] = (out[name] * factor).astype(out[name].dtype)
    return out
```

```python
from contextlib import ExitStack

import concourse.bass as bass
import numpy as np
from concourse import mybir

F32 = mybir.dt.float32
BF16 = mybir.dt.bfloat16
I32 = mybir.dt.int32
U32 = mybir.dt.uint32
ALU = mybir.AluOpType
ACT = mybir.ActivationFunctionType
AX = mybir.AxisListType

P = 128
NK = 77
NH = 16
DH = 16
D = 256
KC = D // P
T = 2
TOK = T * P
E = 8
SW = 80
ROUNDS = 4
SPARE = 18
BANK = 512
SB = 3
ORDER = (8, 0, 1, 2, 3, 4, 5, 6, 7)
EXPERTS = E + 1
LN_EPS = 1e-5


class Signal:

    def __init__(self, sem, per):
        self.sem, self.per = sem, per

    def at(self, b, k=None):
        k = self.per if k is None else max(k, 0)
        return (b + 1) * self.per + k


def xattn_moe_kernel(nc, x, ctx_in, wq, wk, wv, wo, bq, bk, bv, bo, gate_w, lb_bias, w1, w2, cfc, cproj,
                     ident_in, head_of_in, iota_in, keep_in, inv_k_in, out):
    NB = x.shape[0]
    sw_dram = nc.dram_tensor("sw_scratch", [E, TOK], F32, kind="Internal").ap()

    with ExitStack() as stack:
        def sb(name, shape, dt=F32):
            return stack.enter_context(nc.sbuf_tensor(name, shape, dt))

        def ps(name, shape):
            return stack.enter_context(nc.psum_tensor(name, shape, F32))

        signals = []

        def sig(name, per=1):
            signals.append(Signal(stack.enter_context(nc.semaphore(name)), per))
            return signals[-1]

        def plain(name):
            return stack.enter_context(nc.semaphore(name))

        wq_sb, wk_sb, wv_sb, wo_sb = (sb(n, [P, KC, D]) for n in ("wq_sb", "wk_sb", "wv_sb", "wo_sb"))
        w1_sb = sb("w1_sb", [P, E + 1, KC, D])
        w2_sb = sb("w2_sb", [P, E + 1, KC, D])
        gate_sb = sb("gate_sb", [P, KC, E])
        bq_sb, bk_sb = sb("bq_sb", [P, KC]), sb("bk_sb", [P, KC])
        bv_sb = sb("bv_sb", [NK, D])
        bo_sb = sb("bo_sb", [P, D])
        lb_sb = sb("lb_sb", [P, E])
        ident = sb("ident", [P, P])
        head_of = sb("head_of", [P, 8])
        iota = sb("iota", [P, E])
        keep = sb("keep", [P, NH * 8])
        inv_k = sb("inv_k", [P, NH * 8])
        ones = sb("ones", [P, 1])
        half_pow, neg_half_pow = sb("half_pow", [P, T * E]), sb("neg_half_pow", [P, T])

        x_sb = sb("x_sb", [P, 2, T, D])
        ctx_sb = sb("ctx_sb", [NK, D])
        ctxT = sb("ctxT", [P, KC, NK])
        kT = sb("kT", [P, KC, NK])
        k_diag = sb("k_diag", [P, KC, 8, NK])
        v_pad = sb("v_pad", [NK, 2, NH, 2 * DH])
        ln_stats, ln_mv, ln_rstd = sb("ln_stats", [P, T, 6]), sb("ln_mv", [P, T, 2]), sb("ln_rstd", [P, T])
        ln_veps = sb("ln_veps", [P, T])
        xn = sb("xn", [P, T, D])
        xnT = sb("xnT", [P, KC, TOK])
        qT = sb("qT", [P, KC, TOK])
        S = sb("S", [P, 2, T, NH, NK])
        top8 = sb("top8", [P, T, NH, 8])
        csum = sb("csum", [P, T, NH * 8])
        bounds = sb("bounds", [P, T, NH * 8])
        tau = sb("tau", [P, 2, T, NH])
        over = sb("over", [P, T, NH, NK])
        R = sb("R", [P, 2, T, NH, NK])
        signs = sb("signs", [P, T, NH, SW], BF16)
        fold_a, fold_b = sb("fold_a", [P, T, NH, SW // 2], BF16), sb("fold_b", [P, T, NH, SW // 4], BF16)
        fsum, csign = sb("fsum", [P, T, NH]), sb("csign", [P, T, NH])
        den, rden, step = sb("den", [P, T, NH]), sb("rden", [P, T, NH]), sb("step", [P, T, NH])
        spare_f, spare_n, spare_r = (sb(f"spare_{n}", [P, T * NH]) for n in "fnr")
        tol, late, late_any = sb("tol", [P, T * NH]), sb("late", [P, T * NH]), sb("late_any", [P, 1])
        late_count = sb("late_count", [1, 1], I32)
        attnT = sb("attnT", [NK, T, NH, P])
        OT = sb("OT", [P, KC, TOK])
        xb = sb("xb", [P, 2, T, D])

        x1 = sb("x1", [P, 2, T, D])
        f_stats, f_mv, f_rstd = sb("f_stats", [P, T, 6]), sb("f_mv", [P, T, 2]), sb("f_rstd", [P, T])
        f_veps = sb("f_veps", [P, T])
        x1n = sb("x1n", [P, T, D])
        x1nT = sb("x1nT", [P, 2, KC, TOK])
        biased, best = sb("biased", [P, T, E]), sb("best", [P, T, 8])
        best_at, best_f = sb("best_at", [P, T, 8], U32), sb("best_f", [P, T, 2])
        first, chosen = sb("first", [P, T, E]), sb("chosen", [P, T, E])
        sigm, wsel = sb("sigm", [P, T, E]), sb("wsel", [P, T, E])
        wsum, wrec, wnorm = sb("wsum", [P, T]), sb("wrec", [P, T]), sb("wnorm", [P, T, E])
        sw = sb("sw", [P, T, E])
        swT = sb("swT", [E, TOK])
        sw_all = sb("sw_all", [P, E + 1, TOK])
        g = sb("g", [P, 2, KC, TOK])
        hid = sb("hid", [P, 2, KC, TOK])
        y = sb("y", [P, T, D])

        s_ps = ps("s_ps", [P, SB, BANK])
        h_ps = ps("h_ps", [P, 2, KC, TOK])
        y_ps = ps("y_ps", [P, T, D])
        m_ps = ps("m_ps", [P, 2, BANK])

        w_att, w_ffn, consts, spare_step = (plain(n) for n in ("w_att_loaded", "w_ffn_loaded", "consts_set",
                                                               "spare_step"))
        x_loaded = [plain(f"x_loaded_{p}") for p in range(2)]
        ctx_loaded = sig("ctx_loaded", 16)
        sw_stored, sw_spread, out_stored = sig("sw_stored", 16), sig("sw_spread", 16), sig("out_stored", 16)

        ctxT_done, ctxT_taken = sig("ctxT_done"), sig("ctxT_taken")
        k_done, k_taken = sig("k_done"), sig("k_taken")
        v_done, v_taken = sig("v_done"), sig("v_taken", 2)
        xT_done, xT_taken = sig("xT_done", T), sig("xT_taken", T)
        q_done, q_taken = sig("q_done", KC), sig("q_taken", KC)
        o_done, o_taken = sig("o_done", T), sig("o_taken", T)
        late_done, late_taken = sig("late_done"), sig("late_taken")
        wo_done, x1_done = sig("wo_done", T), sig("x1_done", T)
        x1T_done, x1T_taken = sig("x1T_done", T), sig("x1T_taken", T)
        logits_done, logits_biased, logits_sigm = sig("logits_done"), sig("logits_biased"), sig("logits_sigm")
        swT_done, swT_taken = sig("swT_done"), sig("swT_taken")

        k_diag_ready = sig("k_diag_ready")
        s_done, s_taken = sig("s_done", T), sig("s_taken", T)
        veps_ready, rstd_ready, xn_ready = sig("veps_ready", T), sig("rstd_ready"), sig("xn_ready", T)
        ln_chain = sig("ln_chain", 2 * T)
        top_chain = sig("top_chain", 3 * T)
        tau_first, tau_ready = sig("tau_first", T), sig("tau_ready", ROUNDS * T)
        over_ready = sig("over_ready", (ROUNDS + 1) * T)
        relu_done, sign_done = sig("relu_done", (ROUNDS + 1) * T), sig("sign_done", ROUNDS * T)
        f_summed, signs_folded = sig("f_summed", (ROUNDS + 1) * T), sig("signs_folded", ROUNDS * T)
        newton_chain = sig("newton_chain", 5 * ROUNDS * T)
        late_chain, late_known, attn_checked = sig("late_chain", 5), sig("late_known"), sig("attn_checked")
        aT_done, aT_taken = sig("aT_done", 4 * T), sig("aT_taken", 4 * T)
        xb_ready = sig("xb_ready")
        f_chain, f_veps_ready = sig("f_chain", 2 * T), sig("f_veps_ready", T)
        f_rstd_ready, x1n_ready = sig("f_rstd_ready"), sig("x1n_ready", T)
        gate_chain, w_ready, sw_ready = sig("gate_chain", 10), sig("w_ready"), sig("sw_ready")
        l1_done, gated, hid_ready, l2_done = (sig(n, EXPERTS) for n in ("l1_done", "gated", "hid_ready", "l2_done"))
        y_ready = sig("y_ready", T)

        def x_loads(b):
            return 8 * b + 16

        def rt(r, t):
            return r * T + t + 1

        def row(ap, n):
            return ap.rearrange("(a n) -> a n", a=1).broadcast_to([n, ap.shape[0]])

        def chunked(w):
            return w.rearrange("(k p) n -> p k n", p=P)

        waits_stood = {e: plain(f"waits_stood_{n}") for n, e in
                       (("dve", mybir.EngineType.DVE), ("sp", mybir.EngineType.SP))}

        def stand(eng):
            eng.sem_inc(waits_stood[eng.engine], 1)

        block = stack.enter_context(nc.Block())

        N_ATT_LOADS = 4 + 10
        N_CONSTS = 6

        def turns(eng, turn, first=None):
            turn(0, 0, new=True)
            if first is not None:
                first()
            turn(1, 1, new=True, mid=True)
            with eng.Fori(2, NB, 2) as b:
                turn(b, 0, new=True, mid=True, old=True)
                turn(b + 1, 1, new=True, mid=True, old=True)
            turn(NB, 0, mid=True, old=True)
            turn(NB + 1, 1, old=True)

        @block.sync
        def _(sp):
            def load(b, p):
                sp.wait_ge(ctxT_done.sem, ctxT_done.at(b - 1))
                stand(sp)
                sp.dma_start(ctx_sb[:], ctx_in[b]).then_inc(ctx_loaded.sem, 16)
                sp.wait_ge(xn_ready.sem, xn_ready.at(b - 2))
                stand(sp)
                sp.wait_ge(xb_ready.sem, xb_ready.at(b - 2))
                stand(sp)
                sp.dma_start(x_sb[:, p], x[b].rearrange("(t p) d -> p t d", p=P)).then_inc(x_loaded[p], 16)

            def spread_weights(f):
                sp.wait_ge(swT_taken.sem, swT_taken.at(f))
                stand(sp)
                sp.dma_start(sw_dram[:], swT[:]).then_inc(sw_stored.sem, 16)
                sp.wait_ge(sw_stored.sem, sw_stored.at(f))
                stand(sp)
                sp.wait_ge(gated.sem, gated.at(f - 1))
                stand(sp)
                sp.dma_start(sw_all[:, 0:E, :],
                             sw_dram.rearrange("(a e) n -> a (e n)", a=1).broadcast_to([P, E * TOK])
                             ).then_inc(sw_spread.sem, 16)

            def store(f):
                sp.wait_ge(y_ready.sem, y_ready.at(f))
                stand(sp)
                sp.dma_start(out[f].rearrange("(t p) d -> p t d", p=P), y[:]).then_inc(out_stored.sem, 16)

            sp.dma_start(ctx_sb[:], ctx_in[0]).then_inc(ctx_loaded.sem, 16)
            sp.dma_start(x_sb[:, 0], x[0].rearrange("(t p) d -> p t d", p=P)).then_inc(x_loaded[0], 16)
            for dst, src in ((wk_sb, wk), (wv_sb, wv), (wq_sb, wq), (wo_sb, wo)):
                sp.dma_start(dst[:], chunked(src)).then_inc(w_att, 16)
            sp.dma_start(x_sb[:, 1], x[1].rearrange("(t p) d -> p t d", p=P)).then_inc(x_loaded[1], 16)
            sp.wait_ge(ctxT_done.sem, ctxT_done.at(0))
            sp.dma_start(ctx_sb[:], ctx_in[1]).then_inc(ctx_loaded.sem, 16)
            load(2, 0)
            with sp.Fori(2, NB - 2, 2) as b:
                for p in range(2):
                    spread_weights(b + p - 2)
                    load(b + p + 1, 1 - p)
                    store(b + p - 2)
            spread_weights(NB - 4)
            load(NB - 1, 1)
            store(NB - 4)
            for f in (NB - 3, NB - 2, NB - 1):
                spread_weights(f)
                store(f)
            sp.wait_ge(out_stored.sem, out_stored.at(NB - 1))

        @block.gpsimd
        def _(pool):
            for s in signals:
                pool.sem_inc(s.sem, s.per)
            pool.sem_inc(x_loaded[1], 8)
            for t, v in ((ones, 1.0), (half_pow, 0.5), (neg_half_pow, -0.5), (v_pad, 0.0), (signs, 0.0),
                         (sw_all[:, E, :], 1.0)):
                pool.memset(t[:], v).then_inc(consts, 1)
            pool.dma_start(w1_sb[:, 0:E], w1.rearrange("e (k p) n -> p e k n", p=P)).then_inc(w_ffn, 16)
            pool.dma_start(w1_sb[:, E], chunked(cfc)).then_inc(w_ffn, 16)
            pool.dma_start(w2_sb[:, 0:E], w2.rearrange("e (k p) n -> p e k n", p=P)).then_inc(w_ffn, 16)
            pool.dma_start(w2_sb[:, E], chunked(cproj)).then_inc(w_ffn, 16)
            pool.dma_start(gate_sb[:], chunked(gate_w)).then_inc(w_ffn, 16)
            pool.wait_ge(w_att, 16 * N_ATT_LOADS)
            pool.wait_ge(consts, N_CONSTS)

            def new_rstd(b):
                pool.wait_ge(veps_ready.sem, veps_ready.at(b))
                pool.tensor_tensor(ln_rstd[:], ln_veps[:], neg_half_pow[:], ALU.pow).then_inc(rstd_ready.sem, 1)

            def new_keys(b):
                pool.wait_ge(k_taken.sem, k_taken.at(b))
                pool.wait_ge(s_done.sem, s_done.at(b - 1))
                pool.tensor_tensor(k_diag[:],
                                   kT[:].rearrange("p c (o k) -> p c o k", o=1).broadcast_to([P, KC, 8, NK]),
                                   head_of[:].rearrange("p (c h o) -> p c h o", c=1, o=1).broadcast_to([P, KC, 8, NK]),
                                   ALU.mult).then_inc(k_diag_ready.sem, 1)

            def new_residual(b, p):
                pool.wait_ge(x_loaded[p], x_loads(b))
                pool.wait_ge(x1_done.sem, x1_done.at(b - 2))
                pool.tensor_tensor(xb[:, p], x_sb[:, p],
                                   bo_sb[:].rearrange("p (o d) -> p o d", o=1).broadcast_to([P, T, D]),
                                   ALU.add).then_inc(xb_ready.sem, 1)

            def subtract(b, p, r, t):
                if r:
                    pool.wait_ge(tau_ready.sem, tau_ready.at(b, rt(r - 1, t)))
                    pool.wait_ge(sign_done.sem, sign_done.at(b, rt(r - 1, t)))
                else:
                    pool.wait_ge(tau_first.sem, tau_first.at(b, t + 1))
                    pool.wait_ge(relu_done.sem, relu_done.at(b - 1, rt(ROUNDS, t)))
                pool.tensor_tensor(over[:, t], S[:, p, t],
                                   tau[:, p, t].rearrange("p (h o) -> p h o", o=1).broadcast_to([P, NH, NK]),
                                   ALU.subtract).then_inc(over_ready.sem, 1)

            def mid_rstd(m):
                pool.wait_ge(f_veps_ready.sem, f_veps_ready.at(m))
                pool.tensor_tensor(f_rstd[:], f_veps[:], neg_half_pow[:], ALU.pow).then_inc(f_rstd_ready.sem, 1)

            def mid_roots(m):
                pool.wait_ge(w_ready.sem, w_ready.at(m))
                pool.wait_ge(swT_done.sem, swT_done.at(m - 1))
                pool.tensor_tensor(sw[:].rearrange("p t e -> p (t e)"), wnorm[:].rearrange("p t e -> p (t e)"),
                                   half_pow[:], ALU.pow).then_inc(sw_ready.sem, 1)

            def turn(b, p, new=False, mid=False, old=False):
                if new:
                    new_rstd(b)
                if mid:
                    subtract(b - 1, 1 - p, 2, 0)
                    subtract(b - 1, 1 - p, 2, 1)
                if new:
                    new_keys(b)
                if mid:
                    subtract(b - 1, 1 - p, 3, 0)
                    subtract(b - 1, 1 - p, 3, 1)
                if new:
                    new_residual(b, p)
                if mid:
                    subtract(b - 1, 1 - p, 4, 0)
                    subtract(b - 1, 1 - p, 4, 1)
                if new:
                    subtract(b, p, 0, 0)
                    subtract(b, p, 0, 1)
                if new:
                    subtract(b, p, 1, 0)
                    subtract(b, p, 1, 1)
                if mid:
                    mid_rstd(b - 1)
                    mid_roots(b - 1)

            turns(pool, turn)

        @block.scalar
        def _(act):
            for dst, src in ((ident, ident_in), (head_of, head_of_in), (iota, iota_in), (keep, keep_in),
                             (inv_k, inv_k_in), (bq_sb, bq), (bk_sb, bk)):
                act.dma_start(dst[:], src).then_inc(w_att, 16)
            act.dma_start(bv_sb[:], row(bv, NK)).then_inc(w_att, 16)
            act.dma_start(bo_sb[:], row(bo, P)).then_inc(w_att, 16)
            act.dma_start(lb_sb[:], row(lb_bias, P)).then_inc(w_att, 16)
            act.wait_ge(w_att, 16 * N_ATT_LOADS)
            act.activation(sigm[:, 0, :], iota[:], ACT.Sigmoid)

            def pair(bank):
                return m_ps[:, bank, 0:2 * P].rearrange("p (k n) -> p k n", k=2)

            def new_ctx_keys(b):
                act.wait_ge(ctxT_done.sem, ctxT_done.at(b))
                act.wait_ge(v_done.sem, v_done.at(b - 1))
                act.activation(ctxT[:], m_ps[:, 0, 0:KC * NK].rearrange("p (k n) -> p k n", k=KC),
                               ACT.Copy).then_inc(ctxT_taken.sem, 1)
                act.wait_ge(k_done.sem, k_done.at(b))
                act.wait_ge(k_diag_ready.sem, k_diag_ready.at(b - 1))
                for c in range(KC):
                    last = act.activation(kT[:, c], m_ps[:, 1, c * NK:(c + 1) * NK], ACT.Identity,
                                          bias=bk_sb[:, c:c + 1])
                last.then_inc(k_taken.sem, 1)

            def new_turned(b):
                act.wait_ge(q_done.sem, q_done.at(b - 1))
                for t in range(T):
                    act.wait_ge(xT_done.sem, xT_done.at(b, t + 1))
                    act.activation(xnT[:, :, t * P:(t + 1) * P], pair(1 - t), ACT.Copy).then_inc(xT_taken.sem, 1)

            def new_queries(b):
                act.wait_ge(s_done.sem, s_done.at(b - 1))
                for c in range(KC):
                    act.wait_ge(q_done.sem, q_done.at(b, c + 1))
                    act.activation(qT[:, c], m_ps[:, 1 - c, 0:TOK], ACT.Identity, bias=bq_sb[:, c:c + 1]
                                   ).then_inc(q_taken.sem, 1)

            def new_scores(b, p, t):
                act.wait_ge(s_done.sem, s_done.at(b, t + 1))
                act.wait_ge(attn_checked.sem, attn_checked.at(b - 2))
                flat = S[:, p, t].rearrange("p h k -> p (h k)")
                act.activation(flat[:, 0:12 * NK].rearrange("p (a n) -> p a n", a=2), s_ps[:, 0:2, 0:6 * NK],
                               ACT.Copy, scale=DH ** -0.5)
                act.activation(flat[:, 12 * NK:], s_ps[:, 2, 0:4 * NK], ACT.Copy, scale=DH ** -0.5
                               ).then_inc(s_taken.sem, 1)

            def relu_sign(b, p, r, t):
                act.wait_ge(over_ready.sem, over_ready.at(b, rt(r, t)))
                if r:
                    act.wait_ge(f_summed.sem, f_summed.at(b, rt(r - 1, t)))
                else:
                    act.wait_ge(aT_done.sem, aT_done.at(b - 2))
                act.activation(R[:, p, t], over[:, t], ACT.Relu).then_inc(relu_done.sem, 1)
                if r < ROUNDS:
                    if r:
                        act.wait_ge(signs_folded.sem, signs_folded.at(b, rt(r - 1, t)))
                    else:
                        act.wait_ge(signs_folded.sem, signs_folded.at(b - 1, rt(ROUNDS - 1, t)))
                    act.activation(signs[:, t, :, 0:NK], over[:, t], ACT.Sign).then_inc(sign_done.sem, 1)

            def mid_product(m, t):
                for i in range(4):
                    n = 4 * t + i
                    act.wait_ge(aT_done.sem, aT_done.at(m, n + 1))
                    act.wait_ge(o_done.sem, o_done.at(m - 1, t + 1))
                    act.activation(attnT[:, t, 4 * i:4 * i + 4, :],
                                   s_ps[0:NK, n % SB, :].rearrange("p (h n) -> p h n", h=4),
                                   ACT.Copy).then_inc(aT_taken.sem, 1)
                act.wait_ge(o_done.sem, o_done.at(m, t + 1))
                act.wait_ge(wo_done.sem, wo_done.at(m - 1))
                act.activation(OT[:, :, t * P:(t + 1) * P], pair(t), ACT.Copy).then_inc(o_taken.sem, 1)

            def mid_turned(m, p):
                act.wait_ge(l1_done.sem, l1_done.at(m - 2))
                for t in range(T):
                    act.wait_ge(x1T_done.sem, x1T_done.at(m, t + 1))
                    act.activation(x1nT[:, p, :, t * P:(t + 1) * P], pair(t), ACT.Copy).then_inc(x1T_taken.sem, 1)

            def mid_sigmoids(m):
                act.wait_ge(logits_done.sem, logits_done.at(m))
                act.wait_ge(w_ready.sem, w_ready.at(m - 1))
                act.activation(sigm[:].rearrange("p t e -> p (t e)"), m_ps[:, 0, 0:T * E],
                               ACT.Sigmoid).then_inc(logits_sigm.sem, 1)

            def old_roots(f):
                act.wait_ge(swT_done.sem, swT_done.at(f))
                act.wait_ge(sw_stored.sem, sw_stored.at(f - 1))
                act.activation(swT[:], m_ps[0:E, 1, 0:TOK], ACT.Copy).then_inc(swT_taken.sem, 1)

            def old_square(f, i):
                act.wait_ge(gated.sem, gated.at(f, i + 1))
                act.wait_ge(l2_done.sem, l2_done.at(f, i - 1))
                act.activation(hid[:, i % 2], g[:, i % 2], ACT.Square).then_inc(hid_ready.sem, 1)

            def turn(b, p, new=False, mid=False, old=False):
                if old:
                    old_roots(b - 2)
                if new:
                    new_ctx_keys(b)
                if mid:
                    relu_sign(b - 1, 1 - p, 2, 0)
                if new:
                    new_turned(b)
                if mid:
                    relu_sign(b - 1, 1 - p, 2, 1)
                if old:
                    old_square(b - 2, 0)
                if new:
                    new_queries(b)
                if mid:
                    relu_sign(b - 1, 1 - p, 3, 0)
                if new:
                    new_scores(b, p, 0)
                if mid:
                    relu_sign(b - 1, 1 - p, 3, 1)
                if old:
                    old_square(b - 2, 1)
                if new:
                    new_scores(b, p, 1)
                if mid:
                    relu_sign(b - 1, 1 - p, 4, 0)
                if old:
                    old_square(b - 2, 2)
                if mid:
                    relu_sign(b - 1, 1 - p, 4, 1)
                if old:
                    old_square(b - 2, 3)
                if new:
                    relu_sign(b, p, 0, 0)
                if old:
                    old_square(b - 2, 4)
                if new:
                    relu_sign(b, p, 0, 1)
                if mid:
                    mid_product(b - 1, 0)
                if old:
                    old_square(b - 2, 5)
                if mid:
                    mid_product(b - 1, 1)
                if new:
                    relu_sign(b, p, 1, 0)
                if old:
                    old_square(b - 2, 6)
                if new:
                    relu_sign(b, p, 1, 1)
                if old:
                    old_square(b - 2, 7)
                if mid:
                    mid_turned(b - 1, 1 - p)
                    mid_sigmoids(b - 1)
                if old:
                    old_square(b - 2, 8)

            turns(act, turn)

        @block.tensor
        def _(pe):
            pe.wait_ge(w_att, 16 * N_ATT_LOADS)
            pe.wait_ge(consts, N_CONSTS)

            def old_roots(f):
                pe.wait_ge(sw_ready.sem, sw_ready.at(f))
                pe.wait_ge(x1T_taken.sem, x1T_taken.at(f, 2))
                for t in range(T):
                    last = pe.transpose(m_ps[0:E, 1, t * P:(t + 1) * P], sw[:, t, :], ident[:])
                last.then_inc(swT_done.sem, 1)

            def new_keys_values(b, old):
                pe.wait_ge(ctx_loaded.sem, ctx_loaded.at(b))
                for k in range(KC):
                    last = pe.transpose(m_ps[:, 0, k * NK:(k + 1) * NK], ctx_sb[:, k * P:(k + 1) * P],
                                        ident[0:NK, 0:NK])
                last.then_inc(ctxT_done.sem, 1)
                pe.wait_ge(ctxT_taken.sem, ctxT_taken.at(b))
                if old:
                    pe.wait_ge(swT_taken.sem, swT_taken.at(b - 2))
                for c in range(KC):
                    for k in range(KC):
                        last = pe.matmul(m_ps[:, 1, c * NK:(c + 1) * NK], wk_sb[:, k, c * P:(c + 1) * P],
                                         ctxT[:, k, :], start=(k == 0), stop=(k == KC - 1))
                last.then_inc(k_done.sem, 1)
                for k in range(KC):
                    last = pe.matmul(m_ps[0:NK, 0, 0:D], ctxT[:, k, :], wv_sb[:, k, :],
                                     start=(k == 0), stop=(k == KC - 1))
                last.then_inc(v_done.sem, 1)

            def new_turned(b):
                pe.wait_ge(k_taken.sem, k_taken.at(b))
                for t in range(T):
                    pe.wait_ge(xn_ready.sem, xn_ready.at(b, t + 1))
                    if t == 1:
                        pe.wait_ge(v_taken.sem, v_taken.at(b))
                    for k in range(KC):
                        last = pe.transpose(m_ps[:, 1 - t, k * P:(k + 1) * P], xn[:, t, k * P:(k + 1) * P], ident[:])
                    last.then_inc(xT_done.sem, 1)

            def new_queries(b):
                pe.wait_ge(xT_taken.sem, xT_taken.at(b))
                for c in range(KC):
                    for k in range(KC):
                        last = pe.matmul(m_ps[:, 1 - c, 0:TOK], wq_sb[:, k, c * P:(c + 1) * P], xnT[:, k, :],
                                         start=(k == 0), stop=(k == KC - 1))
                    last.then_inc(q_done.sem, 1)

            def new_scores(b, t):
                pe.wait_ge(q_taken.sem, q_taken.at(b))
                pe.wait_ge(k_diag_ready.sem, k_diag_ready.at(b))
                if t:
                    pe.wait_ge(s_taken.sem, s_taken.at(b, t))
                else:
                    pe.wait_ge(aT_taken.sem, aT_taken.at(b - 2))
                for c, h0, n, bank, col in ((0, 0, 6, 0, 0), (0, 6, 2, 1, 0), (1, 0, 4, 1, 2), (1, 4, 4, 2, 0)):
                    last = pe.matmul(s_ps[:, bank, col * NK:(col + n) * NK], qT[:, c, t * P:(t + 1) * P],
                                     k_diag[:, c, h0:h0 + n, :].rearrange("p h k -> p (h k)"),
                                     start=True, stop=True)
                last.then_inc(s_done.sem, 1)

            def mid_late(m):
                pe.wait_ge(late_known.sem, late_known.at(m))
                pe.matmul(m_ps[0:1, 1, 0:1], late_any[:], ones[:], start=True, stop=True).then_inc(late_done.sem, 1)

            def mid_product(m, p, t, new):
                pe.wait_ge(attn_checked.sem, attn_checked.at(m))
                if new:
                    pe.wait_ge(s_taken.sem, s_taken.at(m + 1))
                for i in range(4):
                    n = 4 * t + i
                    pe.wait_ge(aT_taken.sem, aT_taken.at(m, n - SB + 1))
                    for j in range(4):
                        last = pe.transpose(s_ps[0:NK, n % SB, j * P:(j + 1) * P], R[:, p, t, 4 * i + j, :], ident[:])
                    last.then_inc(aT_done.sem, 1)
                for i in range(4):
                    pe.wait_ge(aT_taken.sem, aT_taken.at(m, 4 * t + i + 1))
                    for j in (0, 2, 1, 3):
                        h = 4 * i + j
                        c, quad = h // 8, h % 8 // 2
                        last = pe.matmul(m_ps[32 * quad:32 * quad + 32, t, c * P:(c + 1) * P], v_pad[:, p, h, :],
                                         attnT[:, t, h, :], start=(h % 2 == 0), stop=(h % 2 == 1))
                last.then_inc(o_done.sem, 1)

            def mid_output(m):
                for t in range(T):
                    pe.wait_ge(o_taken.sem, o_taken.at(m, t + 1))
                    for c in range(KC):
                        last = pe.matmul(m_ps[:, t, 0:D], OT[:, c, t * P:(t + 1) * P], wo_sb[:, c, :],
                                         start=(c == 0), stop=(c == KC - 1))
                    last.then_inc(wo_done.sem, 1)

            def mid_turned(m):
                for t in range(T):
                    pe.wait_ge(x1n_ready.sem, x1n_ready.at(m, t + 1))
                    for k in range(KC):
                        last = pe.transpose(m_ps[:, t, k * P:(k + 1) * P], x1n[:, t, k * P:(k + 1) * P], ident[:])
                    last.then_inc(x1T_done.sem, 1)

            def mid_route(m, p):
                pe.wait_ge(x1T_taken.sem, x1T_taken.at(m))
                for t in range(T):
                    for k in range(KC):
                        last = pe.matmul(m_ps[:, 0, t * E:(t + 1) * E], x1nT[:, p, k, t * P:(t + 1) * P],
                                         gate_sb[:, k, :], start=(k == 0), stop=(k == KC - 1))
                last.then_inc(logits_done.sem, 1)

            def layer1(f, p, i):
                e = ORDER[i]
                pe.wait_ge(gated.sem, gated.at(f, i - 1))
                for c in range(KC):
                    for k in range(KC):
                        last = pe.matmul(h_ps[:, i % 2, c, :], w1_sb[:, e, k, c * P:(c + 1) * P], x1nT[:, p, k, :],
                                         start=(k == 0), stop=(k == KC - 1))
                last.then_inc(l1_done.sem, 1)

            def layer2(f, i):
                e = ORDER[i]
                pe.wait_ge(hid_ready.sem, hid_ready.at(f, i + 1))
                if i == 0:
                    pe.wait_ge(y_ready.sem, y_ready.at(f - 1))
                for t in range(T):
                    for c in range(KC):
                        last = pe.matmul(y_ps[:, t, :], hid[:, i % 2, c, t * P:(t + 1) * P], w2_sb[:, e, c, :],
                                         start=(i == 0 and t == 0 and c == 0),
                                         stop=(i == EXPERTS - 1 and c == KC - 1), skip_group_check=True)
                last.then_inc(l2_done.sem, 1)

            def turn(b, p, new=False, mid=False, old=False):
                def expert(i):
                    layer2(b - 2, i)
                    if i + 2 < EXPERTS:
                        layer1(b - 2, p, i + 2)

                if old:
                    layer1(b - 2, p, 0)
                    old_roots(b - 2)
                if new:
                    new_keys_values(b, old)
                if old:
                    layer1(b - 2, p, 1)
                if new:
                    new_turned(b)
                if old:
                    expert(0)
                if new:
                    new_queries(b)
                    new_scores(b, 0)
                if old:
                    expert(1)
                if new:
                    new_scores(b, 1)
                if old:
                    expert(2)
                    expert(3)
                if mid:
                    mid_late(b - 1)
                if old:
                    expert(4)
                if mid:
                    mid_product(b - 1, 1 - p, 0, new)
                if old:
                    expert(5)
                if mid:
                    mid_product(b - 1, 1 - p, 1, new)
                if old:
                    expert(6)
                if mid:
                    mid_output(b - 1)
                if old:
                    expert(7)
                if mid:
                    mid_turned(b - 1)
                    mid_route(b - 1, 1 - p)
                if old:
                    expert(8)

            turns(pe, turn, lambda: pe.wait_ge(w_ffn, 16 * 5))

        @block.vector
        def _(dve):
            dve.wait_ge(w_att, 16 * N_ATT_LOADS)
            dve.wait_ge(consts, N_CONSTS)

            def norm_stats(b, t, src, stats, mv, veps, chain, ready):
                dve.bn_stats(stats[:, t], src).then_inc(chain.sem, 1)
                dve.wait_ge(chain.sem, chain.at(b, 2 * t + 1))
                stand(dve)
                dve.bn_aggr(mv[:, t], stats[:, t]).then_inc(chain.sem, 1)
                dve.wait_ge(chain.sem, chain.at(b, 2 * t + 2))
                dve.tensor_scalar(veps[:, t:t + 1], mv[:, t, 1:2], LN_EPS, None, ALU.add).then_inc(ready.sem, 1)

            def normalise(t, dst, src, mv, rstd, ready):
                dve.tensor_scalar(dst[:, t], src, mv[:, t, 0:1], rstd[:, t:t + 1],
                                  ALU.subtract, ALU.mult).then_inc(ready.sem, 1)

            def new_stats(b, p):
                dve.wait_ge(x_loaded[p], x_loads(b))
                for t in range(T):
                    norm_stats(b, t, x_sb[:, p, t], ln_stats, ln_mv, ln_veps, ln_chain, veps_ready)

            def new_norm(b, p):
                dve.wait_ge(rstd_ready.sem, rstd_ready.at(b))
                dve.wait_ge(xT_done.sem, xT_done.at(b - 1))
                for t in range(T):
                    normalise(t, xn, x_sb[:, p, t], ln_mv, ln_rstd, xn_ready)

            def new_values(b, p):
                dve.wait_ge(v_done.sem, v_done.at(b))
                dve.wait_ge(o_done.sem, o_done.at(b - 2))
                src = m_ps[0:NK, 0, 0:D].rearrange("p (a j d) -> p a j d", j=2, d=DH)
                bias = bv_sb[:].rearrange("p (a j d) -> p a j d", j=2, d=DH)
                for j in range(2):
                    dst = v_pad[:, p].rearrange("p (a j) d -> p a j d", j=2)[:, :, j, j * DH:(j + 1) * DH]
                    dve.tensor_tensor(dst, src[:, :, j, :], bias[:, :, j, :], ALU.add).then_inc(v_taken.sem, 1)

            def new_tau(b, p, t):
                dve.wait_ge(s_taken.sem, s_taken.at(b, t + 1))
                stand(dve)
                for h in range(NH):
                    last = dve.max(top8[:, t, h], S[:, p, t, h])
                last.then_inc(top_chain.sem, 1)
                dve.wait_ge(top_chain.sem, top_chain.at(b, 3 * t + 1))
                top = top8[:, t].rearrange("p h k -> p (h k)")
                dve.tensor_tensor_scan(csum[:, t], keep[:], top, 0.0, ALU.mult, ALU.add).then_inc(top_chain.sem, 1)
                dve.wait_ge(top_chain.sem, top_chain.at(b, 3 * t + 2))
                dve.scalar_tensor_tensor(bounds[:, t], csum[:, t], -1.0, inv_k[:], ALU.add, ALU.mult
                                         ).then_inc(top_chain.sem, 1)
                dve.wait_ge(top_chain.sem, top_chain.at(b, 3 * t + 3))
                dve.tensor_reduce(tau[:, p, t], bounds[:, t].rearrange("p (h k) -> p h k", k=8), AX.X, ALU.max
                                  ).then_inc(tau_first.sem, 1)

            def newton(b, p, r, t, between):
                n0 = 5 * (r * T + t)
                if r == 0:
                    dve.wait_ge(tau_first.sem, tau_first.at(b, t + 1))
                dve.wait_ge(relu_done.sem, relu_done.at(b, rt(r, t)))
                dve.tensor_reduce(fsum[:, t], R[:, p, t], AX.X, ALU.add).then_inc(f_summed.sem, 1)
                dve.wait_ge(sign_done.sem, sign_done.at(b, rt(r, t)))
                dve.tensor_tensor(fold_a[:, t], signs[:, t, :, 0:SW // 2], signs[:, t, :, SW // 2:], ALU.add
                                  ).then_inc(signs_folded.sem, 1)
                between()
                dve.wait_ge(signs_folded.sem, signs_folded.at(b, rt(r, t)))
                dve.tensor_tensor(fold_b[:, t], fold_a[:, t, :, 0:SW // 4], fold_a[:, t, :, SW // 4:], ALU.add
                                  ).then_inc(newton_chain.sem, 1)
                dve.wait_ge(newton_chain.sem, newton_chain.at(b, n0 + 1))
                dve.tensor_reduce(csign[:, t], fold_b[:, t], AX.X, ALU.add).then_inc(newton_chain.sem, 1)
                dve.wait_ge(newton_chain.sem, newton_chain.at(b, n0 + 2))
                dve.tensor_scalar(den[:, t], csign[:, t], float(NK), None, ALU.add).then_inc(newton_chain.sem, 1)
                dve.wait_ge(newton_chain.sem, newton_chain.at(b, n0 + 3))
                dve.reciprocal(rden[:, t], den[:, t]).then_inc(newton_chain.sem, 1)
                dve.wait_ge(newton_chain.sem, newton_chain.at(b, n0 + 4))
                dve.scalar_tensor_tensor(step[:, t], fsum[:, t], -1.0, rden[:, t], ALU.add, ALU.mult
                                         ).then_inc(newton_chain.sem, 1)
                dve.wait_ge(newton_chain.sem, newton_chain.at(b, n0 + 5))
                dve.scalar_tensor_tensor(tau[:, p, t], step[:, t], 2.0, tau[:, p, t], ALU.mult, ALU.add
                                         ).then_inc(tau_ready.sem, 1)

            def flat(ap):
                return ap.rearrange("p t h -> p (t h)")

            def mid_check(m, p):
                tau_m = flat(tau[:, p])
                dve.wait_ge(tau_ready.sem, tau_ready.at(m))
                dve.scalar_tensor_tensor(tol[:], tau_m, -1.0, tau_m, ALU.mult, ALU.max).then_inc(late_chain.sem, 1)
                for t in range(T):
                    dve.wait_ge(relu_done.sem, relu_done.at(m, rt(ROUNDS, t)))
                    dve.tensor_reduce(fsum[:, t], R[:, p, t], AX.X, ALU.add).then_inc(f_summed.sem, 1)
                dve.wait_ge(late_chain.sem, late_chain.at(m, 1))
                dve.tensor_scalar(tol[:], tol[:], 1.0, 5e-7, ALU.max, ALU.mult).then_inc(late_chain.sem, 1)
                dve.wait_ge(late_chain.sem, late_chain.at(m, 2))
                dve.tensor_tensor(tol[:], tol[:], flat(den[:]), ALU.mult).then_inc(late_chain.sem, 1)
                dve.wait_ge(late_chain.sem, late_chain.at(m, 3))
                dve.wait_ge(f_summed.sem, f_summed.at(m))
                dve.scalar_tensor_tensor(late[:], flat(fsum[:]), -1.0, tol[:], ALU.add, ALU.is_gt
                                         ).then_inc(late_chain.sem, 1)
                dve.wait_ge(late_chain.sem, late_chain.at(m, 4))
                dve.tensor_reduce(late_any[:], late[:], AX.X, ALU.add).then_inc(late_known.sem, 1)

            def mid_settle(m, p):
                dve.wait_ge(late_done.sem, late_done.at(m))
                dve.tensor_copy(late_count[:], m_ps[0:1, 1, 0:1]).then_inc(late_taken.sem, 1)
                dve.wait_ge(late_taken.sem, late_taken.at(m))
                stand(dve)
                count = dve.value_load(late_count[0:1, 0:1], min_val=0, max_val=P * T * NH)
                with dve.If(count > 0):
                    spare_steps(p)
                dve.engine_nop().then_inc(late_chain.sem, 1)
                dve.engine_nop().then_inc(attn_checked.sem, 1)

            def spare_steps(p):
                all_s, all_r = (a[:, p].rearrange("p t h k -> p (t h) k") for a in (S, R))
                tau_m = flat(tau[:, p])
                tau_row = tau_m.rearrange("p (h o) -> p h o", o=1).broadcast_to([P, T * NH, NK])
                K = 9
                with dve.Fori(0, SPARE) as s:
                    dve.tensor_tensor(all_r, all_s, tau_row, ALU.subtract).then_inc(spare_step, 1)
                    dve.wait_ge(spare_step, s * K + 1)
                    dve.tensor_scalar(all_r, all_r, 0.0, None, ALU.max).then_inc(spare_step, 1)
                    dve.wait_ge(spare_step, s * K + 2)
                    dve.tensor_reduce(spare_f[:], all_r, AX.X, ALU.add).then_inc(spare_step, 1)
                    dve.wait_ge(spare_step, s * K + 3)
                    dve.tensor_tensor(all_r, all_s, tau_row, ALU.is_gt).then_inc(spare_step, 1)
                    dve.wait_ge(spare_step, s * K + 4)
                    dve.tensor_reduce(spare_n[:], all_r, AX.X, ALU.add).then_inc(spare_step, 1)
                    dve.wait_ge(spare_step, s * K + 5)
                    dve.tensor_scalar(spare_n[:], spare_n[:], 1.0, None, ALU.max).then_inc(spare_step, 1)
                    dve.wait_ge(spare_step, s * K + 6)
                    dve.reciprocal(spare_r[:], spare_n[:]).then_inc(spare_step, 1)
                    dve.wait_ge(spare_step, s * K + 7)
                    dve.scalar_tensor_tensor(spare_f[:], spare_f[:], -1.0, spare_r[:], ALU.add, ALU.mult
                                             ).then_inc(spare_step, 1)
                    dve.wait_ge(spare_step, s * K + 8)
                    dve.tensor_tensor(tau_m, tau_m, spare_f[:], ALU.add).then_inc(spare_step, 1)
                    dve.wait_ge(spare_step, s * K + 9)
                    stand(dve)
                dve.tensor_tensor(all_r, all_s, tau_row, ALU.subtract).then_inc(spare_step, 1)
                dve.wait_ge(spare_step, SPARE * K + 1)
                dve.tensor_scalar(all_r, all_r, 0.0, None, ALU.max).then_inc(spare_step, 1)
                dve.wait_ge(spare_step, SPARE * K + 2)
                dve.sem_clear(spare_step)

            def mid_stats(m, p):
                dve.wait_ge(xb_ready.sem, xb_ready.at(m))
                for t in range(T):
                    dve.wait_ge(wo_done.sem, wo_done.at(m, t + 1))
                    dve.tensor_tensor(x1[:, p, t], m_ps[:, t, 0:D], xb[:, p, t], ALU.add).then_inc(x1_done.sem, 1)
                for t in range(T):
                    dve.wait_ge(x1_done.sem, x1_done.at(m, t + 1))
                    norm_stats(m, t, x1[:, p, t], f_stats, f_mv, f_veps, f_chain, f_veps_ready)

            def mid_norm(m, p):
                dve.wait_ge(f_rstd_ready.sem, f_rstd_ready.at(m))
                for t in range(T):
                    normalise(t, x1n, x1[:, p, t], f_mv, f_rstd, x1n_ready)

            def mid_gate(m):
                dve.wait_ge(logits_sigm.sem, logits_sigm.at(m))
                dve.tensor_tensor(biased[:], m_ps[:, 0, 0:T * E].rearrange("p (t e) -> p t e", t=T),
                                  lb_sb[:].rearrange("p (o e) -> p o e", o=1).broadcast_to([P, T, E]),
                                  ALU.add).then_inc(gate_chain.sem, 1)
                dve.wait_ge(gate_chain.sem, gate_chain.at(m, 1))
                stand(dve)
                for t in range(T):
                    last = dve.max(best[:, t], biased[:, t])
                last.then_inc(gate_chain.sem, 1)
                dve.wait_ge(gate_chain.sem, gate_chain.at(m, 2))
                stand(dve)
                for t in range(T):
                    last = dve.max_index(best_at[:, t], best[:, t], biased[:, t])
                last.then_inc(gate_chain.sem, 1)
                dve.wait_ge(gate_chain.sem, gate_chain.at(m, 3))
                dve.tensor_copy(best_f[:], best_at[:, :, 0:2]).then_inc(gate_chain.sem, 1)
                dve.wait_ge(gate_chain.sem, gate_chain.at(m, 4))
                for t in range(T):
                    last = dve.tensor_scalar(first[:, t], iota[:], best_f[:, t, 0:1], None, ALU.is_equal)
                last.then_inc(gate_chain.sem, 1)
                dve.wait_ge(gate_chain.sem, gate_chain.at(m, 5))
                for t in range(T):
                    last = dve.scalar_tensor_tensor(chosen[:, t], iota[:], best_f[:, t, 1:2], first[:, t],
                                                    ALU.is_equal, ALU.add)
                last.then_inc(gate_chain.sem, 1)
                dve.wait_ge(gate_chain.sem, gate_chain.at(m, 6))
                dve.tensor_tensor(wsel[:], sigm[:], chosen[:], ALU.mult).then_inc(gate_chain.sem, 1)
                dve.wait_ge(gate_chain.sem, gate_chain.at(m, 7))
                dve.tensor_reduce(wsum[:], wsel[:], AX.X, ALU.add).then_inc(gate_chain.sem, 1)
                dve.wait_ge(gate_chain.sem, gate_chain.at(m, 8))
                dve.tensor_scalar(wsum[:], wsum[:], 1e-6, None, ALU.add).then_inc(gate_chain.sem, 1)
                dve.wait_ge(gate_chain.sem, gate_chain.at(m, 9))
                dve.reciprocal(wrec[:], wsum[:]).then_inc(gate_chain.sem, 1)
                dve.wait_ge(gate_chain.sem, gate_chain.at(m, 10))
                dve.wait_ge(sw_ready.sem, sw_ready.at(m - 1))
                dve.tensor_tensor(wnorm[:], wsel[:],
                                  wrec[:].rearrange("p (t o) -> p t o", o=1).broadcast_to([P, T, E]),
                                  ALU.mult).then_inc(w_ready.sem, 1)

            def old_gates(f, i):
                e = ORDER[i]
                if i == 1:
                    dve.wait_ge(sw_spread.sem, sw_spread.at(f))
                dve.wait_ge(l1_done.sem, l1_done.at(f, i + 1))
                dve.wait_ge(hid_ready.sem, hid_ready.at(f, i - 1))
                dve.scalar_tensor_tensor(g[:, i % 2], h_ps[:, i % 2], 0.0,
                                         sw_all[:, e:e + 1, :].broadcast_to([P, KC, TOK]),
                                         ALU.max, ALU.mult).then_inc(gated.sem, 1)

            def old_finish(f, p):
                dve.wait_ge(l2_done.sem, l2_done.at(f))
                dve.wait_ge(out_stored.sem, out_stored.at(f - 1))
                for t in range(T):
                    dve.tensor_tensor(y[:, t], y_ps[:, t, :], x1[:, p, t], ALU.add).then_inc(y_ready.sem, 1)

            def turn(b, p, new=False, mid=False, old=False):
                items = list(range(EXPERTS)) if old else []

                def gates():
                    if items:
                        old_gates(b - 2, items.pop(0))

                def nothing():
                    pass

                if new:
                    new_stats(b, p)
                    new_norm(b, p)
                gates()
                if new:
                    new_values(b, p)
                if mid:
                    newton(b - 1, 1 - p, 2, 0, nothing)
                    newton(b - 1, 1 - p, 2, 1, gates)
                    newton(b - 1, 1 - p, 3, 0, nothing)
                if new:
                    new_tau(b, p, 0)
                if mid:
                    newton(b - 1, 1 - p, 3, 1, gates)
                if new:
                    new_tau(b, p, 1)
                gates()
                if mid:
                    mid_check(b - 1, 1 - p)
                if new:
                    newton(b, p, 0, 0, gates)
                if mid:
                    mid_settle(b - 1, 1 - p)
                if new:
                    newton(b, p, 0, 1, gates)
                gates()
                if new:
                    newton(b, p, 1, 0, nothing)
                while len(items) > 2:
                    gates()
                if mid:
                    mid_stats(b - 1, 1 - p)
                gates()
                if mid:
                    mid_norm(b - 1, 1 - p)
                if new:
                    newton(b, p, 1, 1, gates)
                gates()
                if mid:
                    mid_gate(b - 1)
                while items:
                    gates()
                if old:
                    old_finish(b - 2, p)

            turns(dve, turn)


def kernel(**inputs):
    import concourse.bacc as bacc
    from concourse.bass_utils import run_bass_kernel_spmd

    a = {k.replace("L0_xattn_", "").replace("L0_ffn_", ""): np.ascontiguousarray(v) for k, v in inputs.items()}

    def turned(w):
        return np.ascontiguousarray(np.swapaxes(w, -1, -2))

    arrays = {
        "x": a["x"], "ctx": a["ctx_1024"], "wq": a["Wq"], "wk": a["Wk"], "wv": a["Wv"], "wo": a["Wo"],
        "bq": turned(a["bq"].reshape(KC, P)), "bk": turned(a["bk"].reshape(KC, P)), "bv": a["bv"], "bo": a["bo"],
        "gate_w": turned(a["gate_w"]), "lb_bias": a["lb_bias"], "w1": turned(a["w1"]), "w2": turned(a["w2"]),
        "cfc": turned(a["cfc"]), "cproj": turned(a["cproj"]),
        "ident": np.eye(P, dtype=np.float32),
        "head_of": np.repeat(np.eye(8, dtype=np.float32), DH, axis=0),
        "iota": np.tile(np.arange(E, dtype=np.float32), (P, 1)),
        "keep": np.tile(np.array([0] + [1] * 7, np.float32), (P, NH)),
        "inv_k": np.tile((1.0 / np.arange(1, 9)).astype(np.float32), (P, NH)),
    }
    nc = bacc.Bacc("TRN2", target_bir_lowering=False, num_devices=1)
    args = [nc.dram_tensor(f"in_{n}", v.shape, mybir.dt.from_np(v.dtype), kind="ExternalInput").ap()
            for n, v in arrays.items()]
    out = nc.dram_tensor("out_y", a["x"].shape, F32, kind="ExternalOutput").ap()
    xattn_moe_kernel(nc, *args, out)
    r = run_bass_kernel_spmd(nc, [{f"in_{n}": v for n, v in arrays.items()}], core_ids=[0])
    return r.results[0]["out_y"]
```

```python
from contextlib import ExitStack

import concourse.bass as bass
import numpy as np
from concourse import mybir

F32 = mybir.dt.float32
BF16 = mybir.dt.bfloat16
I32 = mybir.dt.int32
U32 = mybir.dt.uint32
ALU = mybir.AluOpType
ACT = mybir.ActivationFunctionType
AX = mybir.AxisListType

P = 128
NK = 77
NH = 16
DH = 16
D = 256
KC = D // P
T = 2
TOK = T * P
E = 8
SW = 80
ROUNDS = 4
SPARE = 18
BANK = 512
SB = 3
ORDER = (8, 0, 1, 2, 3, 4, 5, 6, 7)
EXPERTS = E + 1
LN_EPS = 1e-5


class Signal:

    def __init__(self, sem, per):
        self.sem, self.per = sem, per

    def at(self, b, k=None):
        k = self.per if k is None else max(k, 0)
        value = (b + 1) * self.per + k
        return max(value, 0) if isinstance(value, int) else value


def xattn_moe_kernel(nc, x, ctx_in, wq, wk, wv, wo, bq, bk, bv, bo, gate_w, lb_bias, w1, w2, cfc, cproj,
                     ident_in, head_of_in, iota_in, keep_in, inv_k_in, out):
    NB = x.shape[0]
    sw_dram = nc.dram_tensor("sw_scratch", [E, TOK], F32, kind="Internal").ap()

    with ExitStack() as stack:
        def sb(name, shape, dt=F32):
            return stack.enter_context(nc.sbuf_tensor(name, shape, dt))

        def ps(name, shape):
            return stack.enter_context(nc.psum_tensor(name, shape, F32))

        signals = []

        def sig(name, per=1):
            signals.append(Signal(stack.enter_context(nc.semaphore(name)), per))
            return signals[-1]

        def plain(name):
            return stack.enter_context(nc.semaphore(name))

        wq_sb, wk_sb, wv_sb, wo_sb = (sb(n, [P, KC, D]) for n in ("wq_sb", "wk_sb", "wv_sb", "wo_sb"))
        w1_sb = sb("w1_sb", [P, E + 1, KC, D])
        w2_sb = sb("w2_sb", [P, E + 1, KC, D])
        gate_sb = sb("gate_sb", [P, KC, E])
        bq_sb, bk_sb = sb("bq_sb", [P, KC]), sb("bk_sb", [P, KC])
        bv_sb = sb("bv_sb", [NK, D])
        bo_sb = sb("bo_sb", [P, D])
        lb_sb = sb("lb_sb", [P, E])
        ident = sb("ident", [P, P])
        head_of = sb("head_of", [P, 8])
        iota = sb("iota", [P, E])
        keep = sb("keep", [P, NH * 8])
        inv_k = sb("inv_k", [P, NH * 8])
        ones = sb("ones", [P, 1])
        half_pow, neg_half_pow = sb("half_pow", [P, T * E]), sb("neg_half_pow", [P, T])

        x_sb = sb("x_sb", [P, 2, T, D])
        ctx_sb = sb("ctx_sb", [NK, D])
        ctxT = sb("ctxT", [P, KC, NK])
        kT = sb("kT", [P, KC, NK])
        k_diag = sb("k_diag", [P, KC, 8, NK])
        v_pad = sb("v_pad", [NK, 2, NH, 2 * DH])
        ln_stats, ln_mv, ln_rstd = sb("ln_stats", [P, T, 6]), sb("ln_mv", [P, T, 2]), sb("ln_rstd", [P, T])
        ln_veps = sb("ln_veps", [P, T])
        xn = sb("xn", [P, T, D])
        xnT = sb("xnT", [P, KC, TOK])
        qT = sb("qT", [P, KC, TOK])
        S = sb("S", [P, 2, T, NH, NK])
        top8 = sb("top8", [P, T, NH, 8])
        csum = sb("csum", [P, T, NH * 8])
        bounds = sb("bounds", [P, T, NH * 8])
        tau = sb("tau", [P, 2, T, NH])
        over = sb("over", [P, 2, T, NH, NK])
        attn = sb("attn", [P, T, NH, NK])
        signs = sb("signs", [P, 2, T, NH, SW], BF16)
        fold_a, fold_b = sb("fold_a", [P, T, NH, SW // 2], BF16), sb("fold_b", [P, T * NH, SW // 4], BF16)
        fsum, asum, den = (sb(n, [P, T * NH]) for n in ("fsum", "asum", "den"))
        rden, step = sb("rden", [P, T * NH]), sb("step", [P, T * NH])
        spare_f, spare_n, spare_r = (sb(f"spare_{n}", [P, T * NH]) for n in "fnr")
        tol, late, late_any = sb("tol", [P, T * NH]), sb("late", [P, T * NH]), sb("late_any", [P, 1])
        late_count = sb("late_count", [1, 1], I32)
        attnT = sb("attnT", [NK, T, NH, P])
        OT = sb("OT", [P, KC, TOK])
        xb = sb("xb", [P, 2, T, D])

        x1 = sb("x1", [P, 2, T, D])
        f_stats, f_mv, f_rstd = sb("f_stats", [P, T, 6]), sb("f_mv", [P, T, 2]), sb("f_rstd", [P, T])
        f_veps = sb("f_veps", [P, T])
        x1n = sb("x1n", [P, T, D])
        x1nT = sb("x1nT", [P, 2, KC, TOK])
        biased, best = sb("biased", [P, T, E]), sb("best", [P, T, 8])
        best_at, best_f = sb("best_at", [P, T, 8], U32), sb("best_f", [P, T, 2])
        first, chosen = sb("first", [P, T, E]), sb("chosen", [P, T, E])
        sigm, wsel = sb("sigm", [P, T, E]), sb("wsel", [P, T, E])
        wsum, wrec, wnorm = sb("wsum", [P, T]), sb("wrec", [P, T]), sb("wnorm", [P, T, E])
        sw = sb("sw", [P, T, E])
        swT = sb("swT", [E, TOK])
        sw_all = sb("sw_all", [P, 2, E + 1, TOK])
        g = sb("g", [P, 2, KC, TOK])
        hid = sb("hid", [P, 2, KC, TOK])
        y = sb("y", [P, T, D])

        s_ps = ps("s_ps", [P, SB, BANK])
        h_ps = ps("h_ps", [P, 2, KC, TOK])
        y_ps = ps("y_ps", [P, T, D])
        m_ps = ps("m_ps", [P, 2, BANK])

        w_att, w_ffn, consts, spare_step = (plain(n) for n in ("w_att_loaded", "w_ffn_loaded", "consts_set",
                                                               "spare_step"))
        x_loaded = [plain(f"x_loaded_{p}") for p in range(2)]
        ctx_loaded = sig("ctx_loaded", 16)
        sw_stored, sw_spread, out_stored = sig("sw_stored", 16), sig("sw_spread", 16), sig("out_stored", 16)

        ctxT_done, ctxT_taken = sig("ctxT_done"), sig("ctxT_taken")
        k_done, k_taken = sig("k_done"), sig("k_taken")
        v_done, v_taken = sig("v_done"), sig("v_taken", 2)
        xT_done, xT_taken = sig("xT_done", T), sig("xT_taken", T)
        q_done, q_taken = sig("q_done", KC), sig("q_taken", KC)
        o_done, o_taken = sig("o_done", T), sig("o_taken", T)
        late_done, late_taken = sig("late_done"), sig("late_taken")
        wo_done, x1_done = sig("wo_done", T), sig("x1_done", T)
        x1T_done, x1T_taken = sig("x1T_done", T), sig("x1T_taken", T)
        logits_done, logits_sigm = sig("logits_done"), sig("logits_sigm")
        swT_done, swT_taken = sig("swT_done"), sig("swT_taken")

        k_diag_ready = sig("k_diag_ready")
        s_done, s_taken = sig("s_done", T), sig("s_taken", T)
        veps_ready, rstd_ready, xn_ready = sig("veps_ready", T), sig("rstd_ready"), sig("xn_ready", T)
        ln_chain = sig("ln_chain", 2 * T)
        top_chain = sig("top_chain", 3 * T)
        tau_first, tau_ready = sig("tau_first", T), sig("tau_ready", ROUNDS)
        over_ready, relu_done, sign_done = (sig(n, ROUNDS * T) for n in ("over_ready", "relu_done", "sign_done"))
        f_summed, signs_folded = sig("f_summed", ROUNDS * T), sig("signs_folded", ROUNDS * T)
        attn_over, attn_ready, attn_summed = (sig(n, T) for n in ("attn_over", "attn_ready", "attn_summed"))
        newton_chain = sig("newton_chain", 4 * ROUNDS)
        late_chain, late_known, attn_checked = sig("late_chain", 4), sig("late_known"), sig("attn_checked")
        aT_done, aT_taken = sig("aT_done", 4 * T), sig("aT_taken", 4 * T)
        xb_ready = sig("xb_ready")
        f_chain, f_veps_ready = sig("f_chain", 2 * T), sig("f_veps_ready", T)
        f_rstd_ready, x1n_ready = sig("f_rstd_ready"), sig("x1n_ready", T)
        gate_chain, w_ready, sw_ready = sig("gate_chain", 10), sig("w_ready"), sig("sw_ready")
        l1_done, gated, hid_ready, l2_done = (sig(n, EXPERTS) for n in ("l1_done", "gated", "hid_ready", "l2_done"))
        y_ready = sig("y_ready", T)

        def x_loads(b):
            return 8 * b + 16

        def rt(r, t):
            return r * T + t + 1

        def row(ap, n):
            return ap.rearrange("(a n) -> a n", a=1).broadcast_to([n, ap.shape[0]])

        def chunked(w):
            return w.rearrange("(k p) n -> p k n", p=P)

        waits_stood = {e: plain(f"waits_stood_{n}") for n, e in
                       (("dve", mybir.EngineType.DVE), ("sp", mybir.EngineType.SP))}

        def stand(eng):
            eng.sem_inc(waits_stood[eng.engine], 1)

        block = stack.enter_context(nc.Block())

        N_ATT_LOADS = 4 + 10
        N_CONSTS = 7

        def turns(eng, turn, first=None):
            turn(0, 0, 1, new=True)
            if first is not None:
                first()
            turn(1, 1, 0, new=True, mid=True)
            turn(2, 0, 1, new=True, mid=True, late=True)
            with eng.Fori(3, NB - 1, 2) as b:
                turn(b, 1, 0, new=True, mid=True, late=True, old=True)
                turn(b + 1, 0, 1, new=True, mid=True, late=True, old=True)
            turn(NB - 1, 1, 0, new=True, mid=True, late=True, old=True)
            turn(NB, 0, 1, mid=True, late=True, old=True)
            turn(NB + 1, 1, 0, late=True, old=True)
            turn(NB + 2, 0, 1, old=True)

        @block.sync
        def _(sp):
            def load(b, p):
                sp.wait_ge(ctxT_done.sem, ctxT_done.at(b - 1))
                stand(sp)
                sp.dma_start(ctx_sb[:], ctx_in[b]).then_inc(ctx_loaded.sem, 16)
                sp.wait_ge(xn_ready.sem, xn_ready.at(b - 2))
                stand(sp)
                sp.wait_ge(xb_ready.sem, xb_ready.at(b - 2))
                stand(sp)
                sp.dma_start(x_sb[:, p], x[b].rearrange("(t p) d -> p t d", p=P)).then_inc(x_loaded[p], 16)

            def spread_weights(f, p):
                sp.wait_ge(swT_taken.sem, swT_taken.at(f))
                stand(sp)
                sp.dma_start(sw_dram[:], swT[:]).then_inc(sw_stored.sem, 16)
                sp.wait_ge(sw_stored.sem, sw_stored.at(f))
                stand(sp)
                sp.wait_ge(gated.sem, gated.at(f - 2))
                stand(sp)
                sp.dma_start(sw_all[:, p, 0:E, :],
                             sw_dram.rearrange("(a e) n -> a (e n)", a=1).broadcast_to([P, E * TOK])
                             ).then_inc(sw_spread.sem, 16)

            def store(f):
                sp.wait_ge(y_ready.sem, y_ready.at(f))
                stand(sp)
                sp.dma_start(out[f].rearrange("(t p) d -> p t d", p=P), y[:]).then_inc(out_stored.sem, 16)

            def turn(b, p, q, new=False, late=False, old=False):
                if new:
                    load(b + 1, q)
                if late:
                    spread_weights(b - 2, p)
                if old:
                    store(b - 3)

            sp.dma_start(ctx_sb[:], ctx_in[0]).then_inc(ctx_loaded.sem, 16)
            sp.dma_start(x_sb[:, 0], x[0].rearrange("(t p) d -> p t d", p=P)).then_inc(x_loaded[0], 16)
            for dst, src in ((wk_sb, wk), (wv_sb, wv), (wq_sb, wq), (wo_sb, wo)):
                sp.dma_start(dst[:], chunked(src)).then_inc(w_att, 16)
            turn(0, 0, 1, new=True)
            turn(1, 1, 0, new=True)
            turn(2, 0, 1, new=True, late=True)
            with sp.Fori(3, NB - 3, 2) as b:
                turn(b, 1, 0, new=True, late=True, old=True)
                turn(b + 1, 0, 1, new=True, late=True, old=True)
            for b in range(NB - 3, NB + 3):
                turn(b, b % 2, 1 - b % 2, new=b < NB - 1, late=b < NB + 2, old=True)
            sp.wait_ge(out_stored.sem, out_stored.at(NB - 1))

        @block.gpsimd
        def _(pool):
            for s in signals:
                pool.sem_inc(s.sem, s.per)
            pool.sem_inc(x_loaded[1], 8)
            for t, v in ((ones, 1.0), (half_pow, 0.5), (neg_half_pow, -0.5), (v_pad, 0.0),
                         (signs[:, :, :, :, NK:SW - 1], 26.0), (signs[:, :, :, :, SW - 1:], 25.0),
                         (sw_all[:, :, E, :], 1.0)):
                pool.memset(t[:], v).then_inc(consts, 1)
            pool.dma_start(w1_sb[:, 0:E], w1.rearrange("e (k p) n -> p e k n", p=P)).then_inc(w_ffn, 16)
            pool.dma_start(w1_sb[:, E], chunked(cfc)).then_inc(w_ffn, 16)
            pool.dma_start(w2_sb[:, 0:E], w2.rearrange("e (k p) n -> p e k n", p=P)).then_inc(w_ffn, 16)
            pool.dma_start(w2_sb[:, E], chunked(cproj)).then_inc(w_ffn, 16)
            pool.dma_start(gate_sb[:], chunked(gate_w)).then_inc(w_ffn, 16)
            pool.wait_ge(w_att, 16 * N_ATT_LOADS)
            pool.wait_ge(consts, N_CONSTS)

            def new_rstd(b):
                pool.wait_ge(veps_ready.sem, veps_ready.at(b))
                pool.tensor_tensor(ln_rstd[:], ln_veps[:], neg_half_pow[:], ALU.pow).then_inc(rstd_ready.sem, 1)

            def new_keys(b):
                pool.wait_ge(k_taken.sem, k_taken.at(b))
                pool.wait_ge(s_done.sem, s_done.at(b - 1))
                pool.tensor_tensor(k_diag[:],
                                   kT[:].rearrange("p c (o k) -> p c o k", o=1).broadcast_to([P, KC, 8, NK]),
                                   head_of[:].rearrange("p (c h o) -> p c h o", c=1, o=1).broadcast_to([P, KC, 8, NK]),
                                   ALU.mult).then_inc(k_diag_ready.sem, 1)

            def new_residual(b, p):
                pool.wait_ge(x_loaded[p], x_loads(b))
                pool.wait_ge(x1_done.sem, x1_done.at(b - 2))
                pool.tensor_tensor(xb[:, p], x_sb[:, p],
                                   bo_sb[:].rearrange("p (o d) -> p o d", o=1).broadcast_to([P, T, D]),
                                   ALU.add).then_inc(xb_ready.sem, 1)

            def minus_tau(dst, p, t):
                return pool.tensor_tensor(dst, S[:, p, t],
                                          tau[:, p, t].rearrange("p (h o) -> p h o", o=1).broadcast_to([P, NH, NK]),
                                          ALU.subtract)

            def subtract(b, p, r, t):
                if r:
                    pool.wait_ge(tau_ready.sem, tau_ready.at(b, r))
                else:
                    pool.wait_ge(tau_first.sem, tau_first.at(b, t + 1))
                    pool.wait_ge(tau_ready.sem, tau_ready.at(b - 2))
                minus_tau(over[:, p, t], p, t).then_inc(over_ready.sem, 1)

            def mid_subtract(m, p, t):
                pool.wait_ge(tau_ready.sem, tau_ready.at(m))
                pool.wait_ge(aT_done.sem, aT_done.at(m - 1))
                minus_tau(attn[:, t], p, t).then_inc(attn_over.sem, 1)

            def late_rstd(m):
                pool.wait_ge(f_veps_ready.sem, f_veps_ready.at(m))
                pool.tensor_tensor(f_rstd[:], f_veps[:], neg_half_pow[:], ALU.pow).then_inc(f_rstd_ready.sem, 1)

            def late_weight_roots(m):
                pool.wait_ge(w_ready.sem, w_ready.at(m))
                pool.wait_ge(swT_done.sem, swT_done.at(m - 1))
                pool.tensor_tensor(sw[:].rearrange("p t e -> p (t e)"), wnorm[:].rearrange("p t e -> p (t e)"),
                                   half_pow[:], ALU.pow).then_inc(sw_ready.sem, 1)

            def turn(b, p, q, new=False, mid=False, late=False, old=False):
                if new:
                    new_rstd(b)
                    new_keys(b)
                if mid:
                    for t in range(T):
                        subtract(b - 1, q, 3, t)
                if new:
                    for t in range(T):
                        subtract(b, p, 0, t)
                if mid:
                    for t in range(T):
                        mid_subtract(b - 1, q, t)
                if new:
                    subtract(b, p, 1, 0)
                if late:
                    late_rstd(b - 2)
                if new:
                    subtract(b, p, 1, 1)
                    new_residual(b, p)
                if late:
                    late_weight_roots(b - 2)
                if new:
                    for t in range(T):
                        subtract(b, p, 2, t)

            turns(pool, turn)

        @block.scalar
        def _(act):
            for dst, src in ((ident, ident_in), (head_of, head_of_in), (iota, iota_in), (keep, keep_in),
                             (inv_k, inv_k_in), (bq_sb, bq), (bk_sb, bk)):
                act.dma_start(dst[:], src).then_inc(w_att, 16)
            act.dma_start(bv_sb[:], row(bv, NK)).then_inc(w_att, 16)
            act.dma_start(bo_sb[:], row(bo, P)).then_inc(w_att, 16)
            act.dma_start(lb_sb[:], row(lb_bias, P)).then_inc(w_att, 16)
            act.wait_ge(w_att, 16 * N_ATT_LOADS)
            act.activation(sigm[:, 0, :], iota[:], ACT.Sigmoid)

            def pair(bank):
                return m_ps[:, bank, 0:2 * P].rearrange("p (k n) -> p k n", k=2)

            def new_context(b):
                act.wait_ge(ctxT_done.sem, ctxT_done.at(b))
                act.wait_ge(v_done.sem, v_done.at(b - 1))
                act.activation(ctxT[:], m_ps[:, 0, 0:KC * NK].rearrange("p (k n) -> p k n", k=KC),
                               ACT.Copy).then_inc(ctxT_taken.sem, 1)

            def new_keys(b):
                act.wait_ge(k_done.sem, k_done.at(b))
                act.wait_ge(k_diag_ready.sem, k_diag_ready.at(b - 1))
                for c in range(KC):
                    last = act.activation(kT[:, c], m_ps[:, 1, c * NK:(c + 1) * NK], ACT.Identity,
                                          bias=bk_sb[:, c:c + 1])
                last.then_inc(k_taken.sem, 1)

            def new_turned(b):
                act.wait_ge(q_done.sem, q_done.at(b - 1))
                for t in range(T):
                    act.wait_ge(xT_done.sem, xT_done.at(b, t + 1))
                    act.activation(xnT[:, :, t * P:(t + 1) * P], pair(1 - t), ACT.Copy).then_inc(xT_taken.sem, 1)

            def new_queries(b):
                act.wait_ge(s_done.sem, s_done.at(b - 1))
                for c in range(KC):
                    act.wait_ge(q_done.sem, q_done.at(b, c + 1))
                    act.activation(qT[:, c], m_ps[:, 1 - c, 0:TOK], ACT.Identity, bias=bq_sb[:, c:c + 1]
                                   ).then_inc(q_taken.sem, 1)

            def new_scores(b, p, t):
                act.wait_ge(s_done.sem, s_done.at(b, t + 1))
                act.wait_ge(attn_checked.sem, attn_checked.at(b - 2))
                flat = S[:, p, t].rearrange("p h k -> p (h k)")
                act.activation(flat[:, 0:12 * NK].rearrange("p (a n) -> p a n", a=2), s_ps[:, 0:2, 0:6 * NK],
                               ACT.Copy, scale=DH ** -0.5)
                act.activation(flat[:, 12 * NK:], s_ps[:, 2, 0:4 * NK], ACT.Copy, scale=DH ** -0.5
                               ).then_inc(s_taken.sem, 1)

            def sign_relu(b, p, r, t):
                act.wait_ge(over_ready.sem, over_ready.at(b, rt(r, t)))
                if r:
                    act.wait_ge(signs_folded.sem, signs_folded.at(b, rt(r - 1, t)))
                else:
                    act.wait_ge(signs_folded.sem, signs_folded.at(b - 2))
                act.activation(signs[:, p, t, :, 0:NK], over[:, p, t], ACT.Sign).then_inc(sign_done.sem, 1)
                act.wait_ge(sign_done.sem, sign_done.at(b, rt(r, t)))
                act.activation(over[:, p, t], over[:, p, t], ACT.Relu).then_inc(relu_done.sem, 1)

            def mid_attention(m, t):
                act.wait_ge(attn_over.sem, attn_over.at(m, t + 1))
                act.activation(attn[:, t], attn[:, t], ACT.Relu).then_inc(attn_ready.sem, 1)

            def late_product(m, t):
                for i in range(4):
                    n = 4 * t + i
                    act.wait_ge(aT_done.sem, aT_done.at(m, n + 1))
                    act.wait_ge(o_done.sem, o_done.at(m - 1, t + 1))
                    act.activation(attnT[:, t, 4 * i:4 * i + 4, :],
                                   s_ps[0:NK, n % SB, :].rearrange("p (h n) -> p h n", h=4),
                                   ACT.Copy).then_inc(aT_taken.sem, 1)
                act.wait_ge(o_done.sem, o_done.at(m, t + 1))
                act.wait_ge(wo_done.sem, wo_done.at(m - 1))
                act.activation(OT[:, :, t * P:(t + 1) * P], pair(t), ACT.Copy).then_inc(o_taken.sem, 1)

            def late_turned(m, p):
                act.wait_ge(l1_done.sem, l1_done.at(m - 2))
                for t in range(T):
                    act.wait_ge(x1T_done.sem, x1T_done.at(m, t + 1))
                    act.activation(x1nT[:, p, :, t * P:(t + 1) * P], pair(t), ACT.Copy).then_inc(x1T_taken.sem, 1)

            def late_sigmoids(m):
                act.wait_ge(logits_done.sem, logits_done.at(m))
                act.wait_ge(w_ready.sem, w_ready.at(m - 1))
                act.activation(sigm[:].rearrange("p t e -> p (t e)"), m_ps[:, 0, 0:T * E],
                               ACT.Sigmoid).then_inc(logits_sigm.sem, 1)

            def late_roots(f):
                act.wait_ge(swT_done.sem, swT_done.at(f))
                act.wait_ge(sw_stored.sem, sw_stored.at(f - 1))
                act.activation(swT[:], m_ps[0:E, 1, 0:TOK], ACT.Copy).then_inc(swT_taken.sem, 1)

            def old_square(f, i):
                act.wait_ge(gated.sem, gated.at(f, i + 1))
                act.wait_ge(l2_done.sem, l2_done.at(f, i - 1))
                act.activation(hid[:, i % 2], g[:, i % 2], ACT.Square).then_inc(hid_ready.sem, 1)

            def turn(b, p, q, new=False, mid=False, late=False, old=False):
                def square(i):
                    if old:
                        old_square(b - 3, i)

                if new:
                    new_context(b)
                    new_keys(b)
                square(0)
                if new:
                    new_turned(b)
                    new_queries(b)
                square(1)
                if new:
                    new_scores(b, p, 0)
                if mid:
                    sign_relu(b - 1, q, 3, 0)
                square(2)
                if new:
                    new_scores(b, p, 1)
                if mid:
                    sign_relu(b - 1, q, 3, 1)
                square(3)
                if late:
                    late_product(b - 2, 0)
                if new:
                    sign_relu(b, p, 0, 0)
                square(4)
                if late:
                    late_product(b - 2, 1)
                if new:
                    sign_relu(b, p, 0, 1)
                square(5)
                if mid:
                    mid_attention(b - 1, 0)
                    mid_attention(b - 1, 1)
                if late:
                    late_turned(b - 2, p)
                square(6)
                if new:
                    sign_relu(b, p, 1, 0)
                square(7)
                if late:
                    late_sigmoids(b - 2)
                if new:
                    sign_relu(b, p, 1, 1)
                square(8)
                if late:
                    late_roots(b - 2)
                if new:
                    sign_relu(b, p, 2, 0)
                    sign_relu(b, p, 2, 1)

            turns(act, turn)

        @block.tensor
        def _(pe):
            pe.wait_ge(w_att, 16 * N_ATT_LOADS)
            pe.wait_ge(consts, N_CONSTS)

            def late_roots(f):
                pe.wait_ge(sw_ready.sem, sw_ready.at(f))
                pe.wait_ge(x1T_taken.sem, x1T_taken.at(f, 2))
                for t in range(T):
                    last = pe.transpose(m_ps[0:E, 1, t * P:(t + 1) * P], sw[:, t, :], ident[:])
                last.then_inc(swT_done.sem, 1)

            def new_context(b):
                pe.wait_ge(ctx_loaded.sem, ctx_loaded.at(b))
                pe.wait_ge(gate_chain.sem, gate_chain.at(b - 3, 1))
                pe.wait_ge(v_taken.sem, v_taken.at(b - 1))
                for k in range(KC):
                    last = pe.transpose(m_ps[:, 0, k * NK:(k + 1) * NK], ctx_sb[:, k * P:(k + 1) * P],
                                        ident[0:NK, 0:NK])
                last.then_inc(ctxT_done.sem, 1)

            def new_keys(b):
                pe.wait_ge(ctxT_taken.sem, ctxT_taken.at(b))
                pe.wait_ge(late_taken.sem, late_taken.at(b - 2))
                for c in range(KC):
                    for k in range(KC):
                        last = pe.matmul(m_ps[:, 1, c * NK:(c + 1) * NK], wk_sb[:, k, c * P:(c + 1) * P],
                                         ctxT[:, k, :], start=(k == 0), stop=(k == KC - 1))
                last.then_inc(k_done.sem, 1)

            def new_values(b, late):
                pe.wait_ge(q_taken.sem, q_taken.at(b))
                if late:
                    pe.wait_ge(x1_done.sem, x1_done.at(b - 2, 1))
                for k in range(KC):
                    last = pe.matmul(m_ps[0:NK, 0, 0:D], ctxT[:, k, :], wv_sb[:, k, :],
                                     start=(k == 0), stop=(k == KC - 1))
                last.then_inc(v_done.sem, 1)

            def new_turned(b):
                pe.wait_ge(k_taken.sem, k_taken.at(b))
                for t in range(T):
                    pe.wait_ge(xn_ready.sem, xn_ready.at(b, t + 1))
                    for k in range(KC):
                        last = pe.transpose(m_ps[:, 1 - t, k * P:(k + 1) * P], xn[:, t, k * P:(k + 1) * P], ident[:])
                    last.then_inc(xT_done.sem, 1)

            def new_queries(b):
                pe.wait_ge(xT_taken.sem, xT_taken.at(b))
                for c in range(KC):
                    for k in range(KC):
                        last = pe.matmul(m_ps[:, 1 - c, 0:TOK], wq_sb[:, k, c * P:(c + 1) * P], xnT[:, k, :],
                                         start=(k == 0), stop=(k == KC - 1))
                    last.then_inc(q_done.sem, 1)

            def new_scores(b, t):
                pe.wait_ge(q_taken.sem, q_taken.at(b))
                pe.wait_ge(k_diag_ready.sem, k_diag_ready.at(b))
                if t:
                    pe.wait_ge(s_taken.sem, s_taken.at(b, t))
                else:
                    pe.wait_ge(aT_taken.sem, aT_taken.at(b - 3))
                for c, h0, n, bank, col in ((0, 0, 6, 0, 0), (0, 6, 2, 1, 0), (1, 0, 4, 1, 2), (1, 4, 4, 2, 0)):
                    last = pe.matmul(s_ps[:, bank, col * NK:(col + n) * NK], qT[:, c, t * P:(t + 1) * P],
                                     k_diag[:, c, h0:h0 + n, :].rearrange("p h k -> p (h k)"),
                                     start=True, stop=True)
                last.then_inc(s_done.sem, 1)

            def late_unsettled(m):
                pe.wait_ge(late_known.sem, late_known.at(m))
                pe.wait_ge(swT_taken.sem, swT_taken.at(m - 1))
                pe.matmul(m_ps[0:1, 1, 0:1], late_any[:], ones[:], start=True, stop=True).then_inc(late_done.sem, 1)

            def late_product(m, p, t, new):
                pe.wait_ge(attn_checked.sem, attn_checked.at(m))
                if new:
                    pe.wait_ge(s_taken.sem, s_taken.at(m + 2))
                else:
                    pe.wait_ge(gate_chain.sem, gate_chain.at(m - 1, 1))
                for i in range(4):
                    n = 4 * t + i
                    pe.wait_ge(aT_taken.sem, aT_taken.at(m, n - SB + 1))
                    for j in range(4):
                        last = pe.transpose(s_ps[0:NK, n % SB, j * P:(j + 1) * P], attn[:, t, 4 * i + j, :], ident[:])
                    last.then_inc(aT_done.sem, 1)
                for i in range(4):
                    pe.wait_ge(aT_taken.sem, aT_taken.at(m, 4 * t + i + 1))
                    for j in (0, 2, 1, 3):
                        h = 4 * i + j
                        c, quad = h // 8, h % 8 // 2
                        last = pe.matmul(m_ps[32 * quad:32 * quad + 32, t, c * P:(c + 1) * P], v_pad[:, p, h, :],
                                         attnT[:, t, h, :], start=(h % 2 == 0), stop=(h % 2 == 1))
                last.then_inc(o_done.sem, 1)

            def late_output(m):
                for t in range(T):
                    pe.wait_ge(o_taken.sem, o_taken.at(m, t + 1))
                    for c in range(KC):
                        last = pe.matmul(m_ps[:, t, 0:D], OT[:, c, t * P:(t + 1) * P], wo_sb[:, c, :],
                                         start=(c == 0), stop=(c == KC - 1))
                    last.then_inc(wo_done.sem, 1)

            def late_turned(m, new):
                if new:
                    pe.wait_ge(v_taken.sem, v_taken.at(m + 2))
                for t in range(T):
                    pe.wait_ge(x1n_ready.sem, x1n_ready.at(m, t + 1))
                    for k in range(KC):
                        last = pe.transpose(m_ps[:, t, k * P:(k + 1) * P], x1n[:, t, k * P:(k + 1) * P], ident[:])
                    last.then_inc(x1T_done.sem, 1)

            def late_route(m, p):
                pe.wait_ge(x1T_taken.sem, x1T_taken.at(m))
                for t in range(T):
                    for k in range(KC):
                        last = pe.matmul(m_ps[:, 0, t * E:(t + 1) * E], x1nT[:, p, k, t * P:(t + 1) * P],
                                         gate_sb[:, k, :], start=(k == 0), stop=(k == KC - 1))
                last.then_inc(logits_done.sem, 1)

            def layer1(f, p, i):
                e = ORDER[i]
                pe.wait_ge(gated.sem, gated.at(f, i - 1))
                for c in range(KC):
                    for k in range(KC):
                        last = pe.matmul(h_ps[:, i % 2, c, :], w1_sb[:, e, k, c * P:(c + 1) * P], x1nT[:, p, k, :],
                                         start=(k == 0), stop=(k == KC - 1))
                last.then_inc(l1_done.sem, 1)

            def layer2(f, i):
                e = ORDER[i]
                pe.wait_ge(hid_ready.sem, hid_ready.at(f, i + 1))
                if i == 0:
                    pe.wait_ge(y_ready.sem, y_ready.at(f - 1))
                for t in range(T):
                    for c in range(KC):
                        last = pe.matmul(y_ps[:, t, :], hid[:, i % 2, c, t * P:(t + 1) * P], w2_sb[:, e, c, :],
                                         start=(i == 0 and t == 0 and c == 0),
                                         stop=(i == EXPERTS - 1 and c == KC - 1), skip_group_check=True)
                last.then_inc(l2_done.sem, 1)

            def turn(b, p, q, new=False, mid=False, late=False, old=False):
                def l1(i):
                    if old:
                        layer1(b - 3, q, i)

                def l2(i):
                    if old:
                        layer2(b - 3, i)

                l1(0)
                if late:
                    late_unsettled(b - 2)
                if new:
                    new_context(b)
                l1(1)
                if new:
                    new_keys(b)
                    new_turned(b)
                l2(0)
                if new:
                    new_queries(b)
                l1(2)
                if new:
                    new_scores(b, 0)
                l2(1)
                l1(3)
                if new:
                    new_scores(b, 1)
                l2(2)
                l1(4)
                if late:
                    late_product(b - 2, p, 0, new)
                l2(3)
                if late:
                    late_product(b - 2, p, 1, new)
                l1(5)
                if late:
                    late_output(b - 2)
                l2(4)
                l1(6)
                if new:
                    new_values(b, late)
                l2(5)
                if late:
                    late_turned(b - 2, new)
                l1(7)
                if late:
                    late_route(b - 2, p)
                l2(6)
                l1(8)
                l2(7)
                if late:
                    late_roots(b - 2)
                l2(8)

            turns(pe, turn, lambda: pe.wait_ge(w_ffn, 16 * 5))

        @block.vector
        def _(dve):
            dve.wait_ge(w_att, 16 * N_ATT_LOADS)
            dve.wait_ge(consts, N_CONSTS)

            def norm_stats(b, t, src, stats, mv, veps, chain, ready):
                dve.bn_stats(stats[:, t], src).then_inc(chain.sem, 1)
                dve.wait_ge(chain.sem, chain.at(b, 2 * t + 1))
                stand(dve)
                dve.bn_aggr(mv[:, t], stats[:, t]).then_inc(chain.sem, 1)
                dve.wait_ge(chain.sem, chain.at(b, 2 * t + 2))
                dve.tensor_scalar(veps[:, t:t + 1], mv[:, t, 1:2], LN_EPS, None, ALU.add).then_inc(ready.sem, 1)

            def normalise(t, dst, src, mv, rstd, ready):
                dve.tensor_scalar(dst[:, t], src, mv[:, t, 0:1], rstd[:, t:t + 1],
                                  ALU.subtract, ALU.mult).then_inc(ready.sem, 1)

            def new_stats(b, p):
                dve.wait_ge(x_loaded[p], x_loads(b))
                for t in range(T):
                    norm_stats(b, t, x_sb[:, p, t], ln_stats, ln_mv, ln_veps, ln_chain, veps_ready)

            def new_norm(b, p):
                dve.wait_ge(rstd_ready.sem, rstd_ready.at(b))
                dve.wait_ge(xT_done.sem, xT_done.at(b - 1))
                for t in range(T):
                    normalise(t, xn, x_sb[:, p, t], ln_mv, ln_rstd, xn_ready)

            def new_values(b, p):
                dve.wait_ge(v_done.sem, v_done.at(b))
                dve.wait_ge(o_done.sem, o_done.at(b - 2))
                src = m_ps[0:NK, 0, 0:D].rearrange("p (a j d) -> p a j d", j=2, d=DH)
                bias = bv_sb[:].rearrange("p (a j d) -> p a j d", j=2, d=DH)
                for j in range(2):
                    dst = v_pad[:, p].rearrange("p (a j) d -> p a j d", j=2)[:, :, j, j * DH:(j + 1) * DH]
                    dve.tensor_tensor(dst, src[:, :, j, :], bias[:, :, j, :], ALU.add).then_inc(v_taken.sem, 1)

            def new_tau(b, p, t):
                dve.wait_ge(s_taken.sem, s_taken.at(b, t + 1))
                stand(dve)
                for h in range(NH):
                    last = dve.max(top8[:, t, h], S[:, p, t, h])
                last.then_inc(top_chain.sem, 1)
                dve.wait_ge(top_chain.sem, top_chain.at(b, 3 * t + 1))
                top = top8[:, t].rearrange("p h k -> p (h k)")
                dve.tensor_tensor_scan(csum[:, t], keep[:], top, 0.0, ALU.mult, ALU.add).then_inc(top_chain.sem, 1)
                dve.wait_ge(top_chain.sem, top_chain.at(b, 3 * t + 2))
                dve.scalar_tensor_tensor(bounds[:, t], csum[:, t], -1.0, inv_k[:], ALU.add, ALU.mult
                                         ).then_inc(top_chain.sem, 1)
                dve.wait_ge(top_chain.sem, top_chain.at(b, 3 * t + 3))
                dve.tensor_reduce(tau[:, p, t], bounds[:, t].rearrange("p (h k) -> p h k", k=8), AX.X, ALU.max
                                  ).then_inc(tau_first.sem, 1)

            def newton(b, p, r, between):
                n0 = 4 * r
                for t in range(T):
                    dve.wait_ge(sign_done.sem, sign_done.at(b, rt(r, t)))
                    dve.tensor_tensor(fold_a[:, t], signs[:, p, t, :, 0:SW // 2], signs[:, p, t, :, SW // 2:], ALU.add
                                      ).then_inc(signs_folded.sem, 1)
                    dve.wait_ge(relu_done.sem, relu_done.at(b, rt(r, t)))
                    dve.tensor_reduce(fsum[:, t * NH:(t + 1) * NH], over[:, p, t], AX.X, ALU.add
                                      ).then_inc(f_summed.sem, 1)
                dve.wait_ge(signs_folded.sem, signs_folded.at(b, rt(r, 1)))
                halves = fold_a[:].rearrange("p t h k -> p (t h) k")
                dve.tensor_tensor(fold_b[:], halves[:, :, 0:SW // 4], halves[:, :, SW // 4:], ALU.add
                                  ).then_inc(newton_chain.sem, 1)
                between()
                dve.wait_ge(newton_chain.sem, newton_chain.at(b, n0 + 1))
                dve.tensor_reduce(den[:], fold_b[:], AX.X, ALU.add).then_inc(newton_chain.sem, 1)
                dve.wait_ge(newton_chain.sem, newton_chain.at(b, n0 + 2))
                dve.reciprocal(rden[:], den[:]).then_inc(newton_chain.sem, 1)
                dve.wait_ge(newton_chain.sem, newton_chain.at(b, n0 + 3))
                dve.scalar_tensor_tensor(step[:], fsum[:], -1.0, rden[:], ALU.add, ALU.mult
                                         ).then_inc(newton_chain.sem, 1)
                dve.wait_ge(newton_chain.sem, newton_chain.at(b, n0 + 4))
                dve.scalar_tensor_tensor(flat(tau[:, p]), step[:], 2.0, flat(tau[:, p]), ALU.mult, ALU.add
                                         ).then_inc(tau_ready.sem, 1)

            def flat(ap):
                return ap.rearrange("p t h -> p (t h)")

            def mid_tolerance(m, p):
                tau_m = flat(tau[:, p])
                dve.wait_ge(tau_ready.sem, tau_ready.at(m))
                dve.scalar_tensor_tensor(tol[:], tau_m, -1.0, tau_m, ALU.mult, ALU.max).then_inc(late_chain.sem, 1)
                dve.wait_ge(late_chain.sem, late_chain.at(m, 1))
                dve.tensor_scalar(tol[:], tol[:], 1.0, 5e-7, ALU.max, ALU.mult).then_inc(late_chain.sem, 1)
                dve.wait_ge(late_chain.sem, late_chain.at(m, 2))
                dve.tensor_tensor(tol[:], tol[:], den[:], ALU.mult).then_inc(late_chain.sem, 1)

            def mid_check(m):
                for t in range(T):
                    dve.wait_ge(attn_ready.sem, attn_ready.at(m, t + 1))
                    dve.tensor_reduce(asum[:, t * NH:(t + 1) * NH], attn[:, t], AX.X, ALU.add
                                      ).then_inc(attn_summed.sem, 1)
                dve.wait_ge(late_chain.sem, late_chain.at(m, 3))
                dve.wait_ge(attn_summed.sem, attn_summed.at(m))
                dve.scalar_tensor_tensor(late[:], asum[:], -1.0, tol[:], ALU.add, ALU.is_gt
                                         ).then_inc(late_chain.sem, 1)
                dve.wait_ge(late_chain.sem, late_chain.at(m, 4))
                dve.tensor_reduce(late_any[:], late[:], AX.X, ALU.add).then_inc(late_known.sem, 1)

            def late_verdict(m):
                dve.wait_ge(late_done.sem, late_done.at(m))
                dve.tensor_copy(late_count[:], m_ps[0:1, 1, 0:1]).then_inc(late_taken.sem, 1)

            def late_settle(m, p):
                dve.wait_ge(late_taken.sem, late_taken.at(m))
                stand(dve)
                count = dve.value_load(late_count[0:1, 0:1], min_val=0, max_val=P * T * NH)
                with dve.If(count > 0):
                    spare_steps(p)
                dve.engine_nop().then_inc(attn_checked.sem, 1)

            def spare_steps(p):
                all_s, all_r = (a.rearrange("p t h k -> p (t h) k") for a in (S[:, p], attn[:]))
                tau_m = flat(tau[:, p])
                tau_row = tau_m.rearrange("p (h o) -> p h o", o=1).broadcast_to([P, T * NH, NK])
                K = 9
                with dve.Fori(0, SPARE) as s:
                    dve.tensor_tensor(all_r, all_s, tau_row, ALU.subtract).then_inc(spare_step, 1)
                    dve.wait_ge(spare_step, s * K + 1)
                    dve.tensor_scalar(all_r, all_r, 0.0, None, ALU.max).then_inc(spare_step, 1)
                    dve.wait_ge(spare_step, s * K + 2)
                    dve.tensor_reduce(spare_f[:], all_r, AX.X, ALU.add).then_inc(spare_step, 1)
                    dve.wait_ge(spare_step, s * K + 3)
                    dve.tensor_tensor(all_r, all_s, tau_row, ALU.is_gt).then_inc(spare_step, 1)
                    dve.wait_ge(spare_step, s * K + 4)
                    dve.tensor_reduce(spare_n[:], all_r, AX.X, ALU.add).then_inc(spare_step, 1)
                    dve.wait_ge(spare_step, s * K + 5)
                    dve.tensor_scalar(spare_n[:], spare_n[:], 1.0, None, ALU.max).then_inc(spare_step, 1)
                    dve.wait_ge(spare_step, s * K + 6)
                    dve.reciprocal(spare_r[:], spare_n[:]).then_inc(spare_step, 1)
                    dve.wait_ge(spare_step, s * K + 7)
                    dve.scalar_tensor_tensor(spare_f[:], spare_f[:], -1.0, spare_r[:], ALU.add, ALU.mult
                                             ).then_inc(spare_step, 1)
                    dve.wait_ge(spare_step, s * K + 8)
                    dve.tensor_tensor(tau_m, tau_m, spare_f[:], ALU.add).then_inc(spare_step, 1)
                    dve.wait_ge(spare_step, s * K + 9)
                    stand(dve)
                dve.tensor_tensor(all_r, all_s, tau_row, ALU.subtract).then_inc(spare_step, 1)
                dve.wait_ge(spare_step, SPARE * K + 1)
                dve.tensor_scalar(all_r, all_r, 0.0, None, ALU.max).then_inc(spare_step, 1)
                dve.wait_ge(spare_step, SPARE * K + 2)
                dve.sem_clear(spare_step)

            def late_stats(m, p):
                dve.wait_ge(xb_ready.sem, xb_ready.at(m))
                for t in range(T):
                    dve.wait_ge(wo_done.sem, wo_done.at(m, t + 1))
                    dve.tensor_tensor(x1[:, p, t], m_ps[:, t, 0:D], xb[:, p, t], ALU.add).then_inc(x1_done.sem, 1)
                for t in range(T):
                    dve.wait_ge(x1_done.sem, x1_done.at(m, t + 1))
                    norm_stats(m, t, x1[:, p, t], f_stats, f_mv, f_veps, f_chain, f_veps_ready)

            def late_norm(m, p):
                dve.wait_ge(f_rstd_ready.sem, f_rstd_ready.at(m))
                for t in range(T):
                    normalise(t, x1n, x1[:, p, t], f_mv, f_rstd, x1n_ready)

            def late_gate(m):
                dve.wait_ge(logits_sigm.sem, logits_sigm.at(m))
                dve.tensor_tensor(biased[:], m_ps[:, 0, 0:T * E].rearrange("p (t e) -> p t e", t=T),
                                  lb_sb[:].rearrange("p (o e) -> p o e", o=1).broadcast_to([P, T, E]),
                                  ALU.add).then_inc(gate_chain.sem, 1)
                dve.wait_ge(gate_chain.sem, gate_chain.at(m, 1))
                stand(dve)
                for t in range(T):
                    last = dve.max(best[:, t], biased[:, t])
                last.then_inc(gate_chain.sem, 1)
                dve.wait_ge(gate_chain.sem, gate_chain.at(m, 2))
                stand(dve)
                for t in range(T):
                    last = dve.max_index(best_at[:, t], best[:, t], biased[:, t])
                last.then_inc(gate_chain.sem, 1)
                dve.wait_ge(gate_chain.sem, gate_chain.at(m, 3))
                dve.tensor_copy(best_f[:], best_at[:, :, 0:2]).then_inc(gate_chain.sem, 1)
                dve.wait_ge(gate_chain.sem, gate_chain.at(m, 4))
                for t in range(T):
                    last = dve.tensor_scalar(first[:, t], iota[:], best_f[:, t, 0:1], None, ALU.is_equal)
                last.then_inc(gate_chain.sem, 1)
                dve.wait_ge(gate_chain.sem, gate_chain.at(m, 5))
                for t in range(T):
                    last = dve.scalar_tensor_tensor(chosen[:, t], iota[:], best_f[:, t, 1:2], first[:, t],
                                                    ALU.is_equal, ALU.add)
                last.then_inc(gate_chain.sem, 1)
                dve.wait_ge(gate_chain.sem, gate_chain.at(m, 6))
                dve.tensor_tensor(wsel[:], sigm[:], chosen[:], ALU.mult).then_inc(gate_chain.sem, 1)
                dve.wait_ge(gate_chain.sem, gate_chain.at(m, 7))
                dve.tensor_reduce(wsum[:], wsel[:], AX.X, ALU.add).then_inc(gate_chain.sem, 1)
                dve.wait_ge(gate_chain.sem, gate_chain.at(m, 8))
                dve.tensor_scalar(wsum[:], wsum[:], 1e-6, None, ALU.add).then_inc(gate_chain.sem, 1)
                dve.wait_ge(gate_chain.sem, gate_chain.at(m, 9))
                dve.reciprocal(wrec[:], wsum[:]).then_inc(gate_chain.sem, 1)
                dve.wait_ge(gate_chain.sem, gate_chain.at(m, 10))
                dve.wait_ge(sw_ready.sem, sw_ready.at(m - 1))
                dve.tensor_tensor(wnorm[:], wsel[:],
                                  wrec[:].rearrange("p (t o) -> p t o", o=1).broadcast_to([P, T, E]),
                                  ALU.mult).then_inc(w_ready.sem, 1)

            def old_gates(f, p, i):
                e = ORDER[i]
                if i == 1:
                    dve.wait_ge(sw_spread.sem, sw_spread.at(f))
                dve.wait_ge(l1_done.sem, l1_done.at(f, i + 1))
                dve.wait_ge(hid_ready.sem, hid_ready.at(f, i - 1))
                dve.scalar_tensor_tensor(g[:, i % 2], h_ps[:, i % 2], 0.0,
                                         sw_all[:, p, e:e + 1, :].broadcast_to([P, KC, TOK]),
                                         ALU.max, ALU.mult).then_inc(gated.sem, 1)

            def old_finish(f, p):
                dve.wait_ge(l2_done.sem, l2_done.at(f))
                dve.wait_ge(out_stored.sem, out_stored.at(f - 1))
                for t in range(T):
                    dve.tensor_tensor(y[:, t], y_ps[:, t, :], x1[:, p, t], ALU.add).then_inc(y_ready.sem, 1)

            def turn(b, p, q, new=False, mid=False, late=False, old=False):
                def gates(i):
                    if old:
                        old_gates(b - 3, q, i)

                if new:
                    new_stats(b, p)
                gates(0)
                if late:
                    late_verdict(b - 2)
                if new:
                    new_norm(b, p)
                if late:
                    late_settle(b - 2, p)
                if mid:
                    newton(b - 1, q, 2, lambda: gates(1))
                else:
                    gates(1)
                gates(2)
                if new:
                    new_tau(b, p, 0)
                gates(3)
                if new:
                    new_tau(b, p, 1)
                if mid:
                    newton(b - 1, q, 3, lambda: gates(4))
                    mid_tolerance(b - 1, q)
                else:
                    gates(4)
                if new:
                    newton(b, p, 0, lambda: gates(5))
                else:
                    gates(5)
                if late:
                    late_stats(b - 2, p)
                if new:
                    new_values(b, p)
                gates(6)
                if late:
                    late_norm(b - 2, p)
                if mid:
                    mid_check(b - 1)
                gates(7)
                if late:
                    late_gate(b - 2)
                if new:
                    newton(b, p, 1, lambda: gates(8))
                else:
                    gates(8)
                if old:
                    old_finish(b - 3, q)

            turns(dve, turn)


def kernel(**inputs):
    import concourse.bacc as bacc
    from concourse.bass_utils import run_bass_kernel_spmd

    a = {k.replace("L0_xattn_", "").replace("L0_ffn_", ""): np.ascontiguousarray(v) for k, v in inputs.items()}

    def turned(w):
        return np.ascontiguousarray(np.swapaxes(w, -1, -2))

    arrays = {
        "x": a["x"], "ctx": a["ctx_1024"], "wq": a["Wq"], "wk": a["Wk"], "wv": a["Wv"], "wo": a["Wo"],
        "bq": turned(a["bq"].reshape(KC, P)), "bk": turned(a["bk"].reshape(KC, P)), "bv": a["bv"], "bo": a["bo"],
        "gate_w": turned(a["gate_w"]), "lb_bias": a["lb_bias"], "w1": turned(a["w1"]), "w2": turned(a["w2"]),
        "cfc": turned(a["cfc"]), "cproj": turned(a["cproj"]),
        "ident": np.eye(P, dtype=np.float32),
        "head_of": np.repeat(np.eye(8, dtype=np.float32), DH, axis=0),
        "iota": np.tile(np.arange(E, dtype=np.float32), (P, 1)),
        "keep": np.tile(np.array([0] + [1] * 7, np.float32), (P, NH)),
        "inv_k": np.tile((1.0 / np.arange(1, 9)).astype(np.float32), (P, NH)),
    }
    nc = bacc.Bacc("TRN2", target_bir_lowering=False, num_devices=1)
    args = [nc.dram_tensor(f"in_{n}", v.shape, mybir.dt.from_np(v.dtype), kind="ExternalInput").ap()
            for n, v in arrays.items()]
    out = nc.dram_tensor("out_y", a["x"].shape, F32, kind="ExternalOutput").ap()
    xattn_moe_kernel(nc, *args, out)
    r = run_bass_kernel_spmd(nc, [{f"in_{n}": v for n, v in arrays.items()}], core_ids=[0])
    return r.results[0]["out_y"]
```

```python
from contextlib import ExitStack

import concourse.bass as bass
import numpy as np
from concourse import mybir

F32 = mybir.dt.float32
BF16 = mybir.dt.bfloat16
I32 = mybir.dt.int32
U32 = mybir.dt.uint32
ALU = mybir.AluOpType
ACT = mybir.ActivationFunctionType
AX = mybir.AxisListType

P = 128
NK = 77
NH = 16
DH = 16
D = 256
KC = D // P
T = 2
TOK = T * P
E = 8
SW = 80
ROUNDS = 4
SPARE = 18
BANK = 512
SB = 3
ORDER = (8, 0, 1, 2, 3, 4, 5, 6, 7)
EXPERTS = E + 1
LN_EPS = 1e-5


class Signal:

    def __init__(self, sem, per):
        self.sem, self.per = sem, per

    def at(self, b, k=None):
        k = self.per if k is None else max(k, 0)
        value = (b + 1) * self.per + k
        return max(value, 0) if isinstance(value, int) else value


def xattn_moe_kernel(nc, x, ctx_in, wq, wk, wv, wo, bq, bk, bv, bo, gate_w, lb_bias, w1, w2, cfc, cproj,
                     ident_in, head_of_in, iota_in, keep_in, inv_k_in, out):
    NB = x.shape[0]
    sw_dram = nc.dram_tensor("sw_scratch", [E, TOK], F32, kind="Internal").ap()

    with ExitStack() as stack:
        def sb(name, shape, dt=F32):
            return stack.enter_context(nc.sbuf_tensor(name, shape, dt))

        def ps(name, shape):
            return stack.enter_context(nc.psum_tensor(name, shape, F32))

        signals = []

        def sig(name, per=1):
            signals.append(Signal(stack.enter_context(nc.semaphore(name)), per))
            return signals[-1]

        def plain(name):
            return stack.enter_context(nc.semaphore(name))

        wq_sb, wk_sb, wv_sb, wo_sb = (sb(n, [P, KC, D]) for n in ("wq_sb", "wk_sb", "wv_sb", "wo_sb"))
        w1_sb = sb("w1_sb", [P, E + 1, KC, D])
        w2_sb = sb("w2_sb", [P, E + 1, KC, D])
        gate_sb = sb("gate_sb", [P, KC, E])
        bq_sb, bk_sb = sb("bq_sb", [P, KC]), sb("bk_sb", [P, KC])
        bv_sb = sb("bv_sb", [NK, D])
        bo_sb = sb("bo_sb", [P, D])
        lb_sb = sb("lb_sb", [P, E])
        ident = sb("ident", [P, P])
        head_of = sb("head_of", [P, 8])
        iota = sb("iota", [P, E])
        keep = sb("keep", [P, NH * 8])
        inv_k = sb("inv_k", [P, NH * 8])
        ones = sb("ones", [P, 1])
        half_pow, neg_half_pow = sb("half_pow", [P, T * E]), sb("neg_half_pow", [P, T])

        x_sb = sb("x_sb", [P, 2, T, D])
        ctx_sb = sb("ctx_sb", [NK, D])
        ctxT = sb("ctxT", [P, KC, NK])
        kT = sb("kT", [P, KC, NK])
        k_diag = sb("k_diag", [P, KC, 8, NK])
        v_pad = sb("v_pad", [NK, 2, NH, 2 * DH])
        ln_stats, ln_mv, ln_rstd = sb("ln_stats", [P, T, 6]), sb("ln_mv", [P, T, 2]), sb("ln_rstd", [P, T])
        ln_veps, ln_minus, ln_shift = (sb(f"ln_{n}", [P, T]) for n in ("veps", "minus", "shift"))
        xn = sb("xn", [P, T, D])
        xnT = sb("xnT", [P, KC, TOK])
        qT = sb("qT", [P, KC, TOK])
        S = sb("S", [P, 2, T, NH, NK])
        top8 = sb("top8", [P, T, NH, 8])
        csum = sb("csum", [P, T, NH * 8])
        bounds = sb("bounds", [P, T, NH * 8])
        tau = sb("tau", [P, 2, T, NH])
        over = sb("over", [P, 2, T, NH, NK])
        attn = sb("attn", [P, T, NH, NK])
        signs = sb("signs", [P, 2, T, NH, SW], BF16)
        fold_a, fold_b = sb("fold_a", [P, T, NH, SW // 2], BF16), sb("fold_b", [P, T * NH, SW // 4], BF16)
        fsum, den = sb("fsum", [P, T * NH]), sb("den", [P, T * NH])
        rden, step = sb("rden", [P, T * NH]), sb("step", [P, T * NH])
        spare_f, spare_n, spare_r = (sb(f"spare_{n}", [P, T * NH]) for n in "fnr")
        tol, asum, unsettled = (sb(n, [P, T * NH]) for n in ("tol", "asum", "unsettled"))
        unsettled_any = sb("unsettled_any", [P, 1])
        unsettled_count = sb("unsettled_count", [1, 1], I32)
        attnT = sb("attnT", [NK, T, NH, P])
        OT = sb("OT", [P, KC, TOK])
        xb = sb("xb", [P, 2, T, D])

        x1 = sb("x1", [P, 2, T, D])
        f_stats, f_mv, f_rstd = sb("f_stats", [P, T, 6]), sb("f_mv", [P, T, 2]), sb("f_rstd", [P, T])
        f_veps, f_minus, f_shift = (sb(f"f_{n}", [P, T]) for n in ("veps", "minus", "shift"))
        x1n = sb("x1n", [P, T, D])
        x1nT = sb("x1nT", [P, 2, KC, TOK])
        biased, best = sb("biased", [P, T, E]), sb("best", [P, T, 8])
        best_at, best_f = sb("best_at", [P, T, 8], U32), sb("best_f", [P, T, 2])
        first, chosen = sb("first", [P, T, E]), sb("chosen", [P, T, E])
        sigm, wsel = sb("sigm", [P, T, E]), sb("wsel", [P, T, E])
        wsum, wrec, wnorm = sb("wsum", [P, T]), sb("wrec", [P, T]), sb("wnorm", [P, T, E])
        sw = sb("sw", [P, T, E])
        swT = sb("swT", [E, TOK])
        sw_all = sb("sw_all", [P, 2, E, TOK])
        g = sb("g", [P, 2, KC, TOK])
        hid = sb("hid", [P, 2, KC, TOK])
        y = sb("y", [P, T, D])

        s_ps = ps("s_ps", [P, SB, BANK])
        h_ps = ps("h_ps", [P, 2, KC, TOK])
        y_ps = ps("y_ps", [P, T, D])
        m_ps = ps("m_ps", [P, 2, BANK])

        w_att, w_ffn, consts, spare_step = (plain(n) for n in ("w_att_loaded", "w_ffn_loaded", "consts_set",
                                                               "spare_step"))
        x_loaded = [plain(f"x_loaded_{p}") for p in range(2)]
        ctx_loaded = sig("ctx_loaded", 16)
        sw_stored, sw_spread, out_stored = sig("sw_stored", 16), sig("sw_spread", 16), sig("out_stored", 16)

        ctxT_done, ctxT_taken = sig("ctxT_done"), sig("ctxT_taken")
        k_done, k_taken = sig("k_done"), sig("k_taken")
        v_done, v_taken = sig("v_done"), sig("v_taken", 2)
        xT_done, xT_taken = sig("xT_done", T), sig("xT_taken", T)
        q_done, q_taken = sig("q_done", KC), sig("q_taken", KC)
        o_done, o_taken = sig("o_done", T), sig("o_taken", T)
        count_done, count_taken = sig("count_done"), sig("count_taken")
        wo_done, x1_done = sig("wo_done", T), sig("x1_done", T)
        x1T_done, x1T_taken = sig("x1T_done", T), sig("x1T_taken", T)
        logits_done, logits_sigm = sig("logits_done"), sig("logits_sigm")
        swT_done, swT_taken = sig("swT_done"), sig("swT_taken")

        k_diag_ready = sig("k_diag_ready")
        s_done, s_taken = sig("s_done", T), sig("s_taken", T)
        veps_ready, rstd_ready, shift_ready = sig("veps_ready", T), sig("rstd_ready"), sig("shift_ready")
        xn_ready = sig("xn_ready", T)
        ln_chain = sig("ln_chain", 2 * T)
        top_chain = sig("top_chain", 3 * T)
        tau_first, tau_ready = sig("tau_first", T), sig("tau_ready", ROUNDS)
        over_ready, relu_done, sign_done = (sig(n, ROUNDS * T) for n in ("over_ready", "relu_done", "sign_done"))
        f_summed, signs_folded = sig("f_summed", ROUNDS * T), sig("signs_folded", ROUNDS * T)
        attn_over, attn_ready, attn_summed = (sig(n, T) for n in ("attn_over", "attn_ready", "attn_summed"))
        newton_chain = sig("newton_chain", 4 * ROUNDS)
        check_chain, unsettled_known, attn_checked = sig("check_chain", 4), sig("unsettled_known"), sig("attn_checked")
        aT_done, aT_taken = sig("aT_done", 4 * T), sig("aT_taken", 4 * T)
        xb_ready = sig("xb_ready")
        f_chain, f_veps_ready = sig("f_chain", 2 * T), sig("f_veps_ready", T)
        f_rstd_ready, f_shift_ready, x1n_ready = sig("f_rstd_ready"), sig("f_shift_ready"), sig("x1n_ready", T)
        gate_chain, w_ready, sw_ready = sig("gate_chain", 10), sig("w_ready"), sig("sw_ready")
        l1_done, gated, hid_ready, l2_done = (sig(n, EXPERTS) for n in ("l1_done", "gated", "hid_ready", "l2_done"))
        y_ready = sig("y_ready", T)

        def x_loads(b):
            return 8 * b + 16

        def rt(r, t):
            return r * T + t + 1

        def row(ap, n):
            return ap.rearrange("(a n) -> a n", a=1).broadcast_to([n, ap.shape[0]])

        def chunked(w):
            return w.rearrange("(k p) n -> p k n", p=P)

        waits_stood = {e: plain(f"waits_stood_{n}") for n, e in
                       (("dve", mybir.EngineType.DVE), ("sp", mybir.EngineType.SP))}

        def stand(eng):
            eng.sem_inc(waits_stood[eng.engine], 1)

        block = stack.enter_context(nc.Block())

        N_ATT_LOADS = 4 + 10
        N_CONSTS = 6

        def turns(eng, turn, first=None):
            if first is not None:
                first()
            turn(0, 0, 1, new=True)
            turn(1, 1, 0, new=True, mid=True)
            turn(2, 0, 1, new=True, mid=True, late=True)
            with eng.Fori(3, NB - 1, 2) as b:
                turn(b, 1, 0, new=True, mid=True, late=True, old=True)
                turn(b + 1, 0, 1, new=True, mid=True, late=True, old=True)
            turn(NB - 1, 1, 0, new=True, mid=True, late=True, old=True, ahead=False)
            turn(NB, 0, 1, mid=True, late=True, old=True)
            turn(NB + 1, 1, 0, late=True, old=True)
            turn(NB + 2, 0, 1, old=True)

        @block.sync
        def _(sp):
            def load_context(b):
                sp.wait_ge(ctxT_done.sem, ctxT_done.at(b - 1))
                stand(sp)
                sp.dma_start(ctx_sb[:], ctx_in[b]).then_inc(ctx_loaded.sem, 16)

            def load_x(b, p):
                sp.wait_ge(xn_ready.sem, xn_ready.at(b - 2))
                stand(sp)
                sp.wait_ge(xb_ready.sem, xb_ready.at(b - 2))
                stand(sp)
                sp.dma_start(x_sb[:, p], x[b].rearrange("(t p) d -> p t d", p=P)).then_inc(x_loaded[p], 16)

            def spread_weights(f, p):
                sp.wait_ge(swT_taken.sem, swT_taken.at(f))
                stand(sp)
                sp.dma_start(sw_dram[:], swT[:]).then_inc(sw_stored.sem, 16)
                sp.wait_ge(sw_stored.sem, sw_stored.at(f))
                stand(sp)
                sp.wait_ge(gated.sem, gated.at(f - 2))
                stand(sp)
                sp.dma_start(sw_all[:, p],
                             sw_dram.rearrange("(a e) n -> a (e n)", a=1).broadcast_to([P, E * TOK])
                             ).then_inc(sw_spread.sem, 16)

            def store(f):
                sp.wait_ge(y_ready.sem, y_ready.at(f))
                stand(sp)
                sp.dma_start(out[f].rearrange("(t p) d -> p t d", p=P), y[:]).then_inc(out_stored.sem, 16)

            def turn(b, p, q, new=False, late=False, old=False):
                if new:
                    load_context(b + 1)
                    load_x(b + 2, p)
                if late:
                    spread_weights(b - 2, p)
                if old:
                    store(b - 3)

            sp.dma_start(ctx_sb[:], ctx_in[0]).then_inc(ctx_loaded.sem, 16)
            sp.dma_start(x_sb[:, 0], x[0].rearrange("(t p) d -> p t d", p=P)).then_inc(x_loaded[0], 16)
            for dst, src in ((wk_sb, wk), (wv_sb, wv), (wq_sb, wq), (wo_sb, wo)):
                sp.dma_start(dst[:], chunked(src)).then_inc(w_att, 16)
            sp.dma_start(x_sb[:, 1], x[1].rearrange("(t p) d -> p t d", p=P)).then_inc(x_loaded[1], 16)
            turn(0, 0, 1, new=True)
            turn(1, 1, 0, new=True)
            turn(2, 0, 1, new=True, late=True)
            with sp.Fori(3, NB - 3, 2) as b:
                turn(b, 1, 0, new=True, late=True, old=True)
                turn(b + 1, 0, 1, new=True, late=True, old=True)
            turn(NB - 3, 1, 0, new=True, late=True, old=True)
            load_context(NB - 1)
            for b in range(NB - 2, NB + 3):
                turn(b, b % 2, 1 - b % 2, late=b < NB + 2, old=True)
            sp.wait_ge(out_stored.sem, out_stored.at(NB - 1))

        @block.gpsimd
        def _(pool):
            for s in signals:
                pool.sem_inc(s.sem, s.per)
            pool.sem_inc(x_loaded[1], 8)
            for t, v in ((ones, 1.0), (half_pow, 0.5), (neg_half_pow, -0.5)):
                pool.memset(t[:], v).then_inc(consts, 1)
            pool.wait_ge(w_att, 16 * N_ATT_LOADS)
            pool.dma_start(w1_sb[:, 0:E], w1.rearrange("e (k p) n -> p e k n", p=P)).then_inc(w_ffn, 16)
            pool.dma_start(w1_sb[:, E], chunked(cfc)).then_inc(w_ffn, 16)
            pool.dma_start(w2_sb[:, 0:E], w2.rearrange("e (k p) n -> p e k n", p=P)).then_inc(w_ffn, 16)
            pool.dma_start(w2_sb[:, E], chunked(cproj)).then_inc(w_ffn, 16)
            pool.dma_start(gate_sb[:], chunked(gate_w)).then_inc(w_ffn, 16)
            pool.wait_ge(consts, N_CONSTS)

            def new_rstd(b):
                pool.wait_ge(veps_ready.sem, veps_ready.at(b))
                pool.wait_ge(xn_ready.sem, xn_ready.at(b - 1))
                pool.tensor_tensor(ln_rstd[:], ln_veps[:], neg_half_pow[:], ALU.pow).then_inc(rstd_ready.sem, 1)
                pool.wait_ge(rstd_ready.sem, rstd_ready.at(b))
                pool.tensor_tensor(ln_shift[:], ln_minus[:], ln_rstd[:], ALU.mult).then_inc(shift_ready.sem, 1)

            def new_keys(b):
                pool.wait_ge(k_taken.sem, k_taken.at(b))
                pool.wait_ge(s_done.sem, s_done.at(b - 1))
                pool.tensor_tensor(k_diag[:],
                                   kT[:].rearrange("p c (o k) -> p c o k", o=1).broadcast_to([P, KC, 8, NK]),
                                   head_of[:].rearrange("p (c h o) -> p c h o", c=1, o=1).broadcast_to([P, KC, 8, NK]),
                                   ALU.mult).then_inc(k_diag_ready.sem, 1)

            def new_residual(b, p):
                pool.wait_ge(x_loaded[p], x_loads(b))
                pool.wait_ge(x1_done.sem, x1_done.at(b - 2))
                pool.tensor_tensor(xb[:, p], x_sb[:, p],
                                   bo_sb[:].rearrange("p (o d) -> p o d", o=1).broadcast_to([P, T, D]),
                                   ALU.add).then_inc(xb_ready.sem, 1)

            def minus_tau(dst, p, t):
                return pool.tensor_tensor(dst, S[:, p, t],
                                          tau[:, p, t].rearrange("p (h o) -> p h o", o=1).broadcast_to([P, NH, NK]),
                                          ALU.subtract)

            def subtract(b, p, r, t):
                if r:
                    pool.wait_ge(tau_ready.sem, tau_ready.at(b, r))
                else:
                    pool.wait_ge(tau_first.sem, tau_first.at(b, t + 1))
                    pool.wait_ge(tau_ready.sem, tau_ready.at(b - 2))
                minus_tau(over[:, p, t], p, t).then_inc(over_ready.sem, 1)

            def mid_subtract(m, p, t):
                pool.wait_ge(tau_ready.sem, tau_ready.at(m))
                pool.wait_ge(aT_done.sem, aT_done.at(m - 1))
                minus_tau(attn[:, t], p, t).then_inc(attn_over.sem, 1)

            def late_rstd(m):
                pool.wait_ge(f_veps_ready.sem, f_veps_ready.at(m))
                pool.wait_ge(x1n_ready.sem, x1n_ready.at(m - 1))
                pool.tensor_tensor(f_rstd[:], f_veps[:], neg_half_pow[:], ALU.pow).then_inc(f_rstd_ready.sem, 1)
                pool.wait_ge(f_rstd_ready.sem, f_rstd_ready.at(m))
                pool.tensor_tensor(f_shift[:], f_minus[:], f_rstd[:], ALU.mult).then_inc(f_shift_ready.sem, 1)

            def late_weight_roots(m):
                pool.wait_ge(w_ready.sem, w_ready.at(m))
                pool.wait_ge(swT_done.sem, swT_done.at(m - 1))
                pool.tensor_tensor(sw[:].rearrange("p t e -> p (t e)"), wnorm[:].rearrange("p t e -> p (t e)"),
                                   half_pow[:], ALU.pow).then_inc(sw_ready.sem, 1)

            def turn(b, p, q, new=False, mid=False, late=False, old=False, ahead=True):
                if new:
                    new_keys(b)
                if mid:
                    for t in range(T):
                        subtract(b - 1, q, 2, t)
                if new and ahead:
                    new_rstd(b + 1)
                if mid:
                    for t in range(T):
                        subtract(b - 1, q, 3, t)
                if new:
                    for t in range(T):
                        subtract(b, p, 0, t)
                if mid:
                    for t in range(T):
                        mid_subtract(b - 1, q, t)
                if late:
                    late_rstd(b - 2)
                if new:
                    new_residual(b, p)
                    for t in range(T):
                        subtract(b, p, 1, t)
                if late:
                    late_weight_roots(b - 2)

            turns(pool, turn, lambda: new_rstd(0))

        @block.scalar
        def _(act):
            for dst, src in ((ident, ident_in), (head_of, head_of_in), (iota, iota_in), (keep, keep_in),
                             (inv_k, inv_k_in), (bq_sb, bq), (bk_sb, bk)):
                act.dma_start(dst[:], src).then_inc(w_att, 16)
            act.dma_start(bv_sb[:], row(bv, NK)).then_inc(w_att, 16)
            act.dma_start(bo_sb[:], row(bo, P)).then_inc(w_att, 16)
            act.dma_start(lb_sb[:], row(lb_bias, P)).then_inc(w_att, 16)
            act.wait_ge(w_att, 16 * N_ATT_LOADS)
            act.activation(sigm[:, 0, :], iota[:], ACT.Sigmoid)

            def pair(bank):
                return m_ps[:, bank, 0:2 * P].rearrange("p (k n) -> p k n", k=2)

            def new_norm(b, p):
                act.wait_ge(shift_ready.sem, shift_ready.at(b))
                act.wait_ge(xT_done.sem, xT_done.at(b - 1))
                for t in range(T):
                    act.activation(xn[:, t], x_sb[:, p, t], ACT.Identity, bias=ln_shift[:, t:t + 1],
                                   scale=ln_rstd[:, t:t + 1]).then_inc(xn_ready.sem, 1)

            def late_norm(m, p):
                act.wait_ge(f_shift_ready.sem, f_shift_ready.at(m))
                act.wait_ge(x1T_done.sem, x1T_done.at(m - 1))
                for t in range(T):
                    act.activation(x1n[:, t], x1[:, p, t], ACT.Identity, bias=f_shift[:, t:t + 1],
                                   scale=f_rstd[:, t:t + 1]).then_inc(x1n_ready.sem, 1)

            def new_context(b):
                act.wait_ge(ctxT_done.sem, ctxT_done.at(b))
                act.wait_ge(v_done.sem, v_done.at(b - 1))
                act.activation(ctxT[:], m_ps[:, 0, 0:KC * NK].rearrange("p (k n) -> p k n", k=KC),
                               ACT.Copy).then_inc(ctxT_taken.sem, 1)

            def new_keys(b):
                act.wait_ge(k_done.sem, k_done.at(b))
                act.wait_ge(k_diag_ready.sem, k_diag_ready.at(b - 1))
                for c in range(KC):
                    last = act.activation(kT[:, c], m_ps[:, 1, c * NK:(c + 1) * NK], ACT.Identity,
                                          bias=bk_sb[:, c:c + 1])
                last.then_inc(k_taken.sem, 1)

            def new_turned(b, t):
                act.wait_ge(q_done.sem, q_done.at(b - 1))
                act.wait_ge(xT_done.sem, xT_done.at(b, t + 1))
                act.activation(xnT[:, :, t * P:(t + 1) * P], pair(t), ACT.Copy).then_inc(xT_taken.sem, 1)

            def new_queries(b):
                act.wait_ge(s_done.sem, s_done.at(b - 1))
                for c in range(KC):
                    act.wait_ge(q_done.sem, q_done.at(b, c + 1))
                    act.activation(qT[:, c], m_ps[:, c, 0:TOK], ACT.Identity, bias=bq_sb[:, c:c + 1]
                                   ).then_inc(q_taken.sem, 1)

            def new_scores(b, p, t):
                act.wait_ge(s_done.sem, s_done.at(b, t + 1))
                act.wait_ge(attn_checked.sem, attn_checked.at(b - 2))
                flat = S[:, p, t].rearrange("p h k -> p (h k)")
                act.activation(flat[:, 0:12 * NK].rearrange("p (a n) -> p a n", a=2), s_ps[:, 0:2, 0:6 * NK],
                               ACT.Copy, scale=DH ** -0.5)
                act.activation(flat[:, 12 * NK:], s_ps[:, 2, 0:4 * NK], ACT.Copy, scale=DH ** -0.5
                               ).then_inc(s_taken.sem, 1)

            def sign_relu(b, p, r, t):
                act.wait_ge(over_ready.sem, over_ready.at(b, rt(r, t)))
                if r:
                    act.wait_ge(signs_folded.sem, signs_folded.at(b, rt(r - 1, t)))
                else:
                    act.wait_ge(signs_folded.sem, signs_folded.at(b - 2))
                act.activation(signs[:, p, t, :, 0:NK], over[:, p, t], ACT.Sign).then_inc(sign_done.sem, 1)
                act.wait_ge(sign_done.sem, sign_done.at(b, rt(r, t)))
                act.activation(over[:, p, t], over[:, p, t], ACT.Relu).then_inc(relu_done.sem, 1)

            def mid_attention(m, t):
                act.wait_ge(attn_over.sem, attn_over.at(m, t + 1))
                act.activation(attn[:, t], attn[:, t], ACT.Relu).then_inc(attn_ready.sem, 1)

            def late_product(m, t):
                for i in range(4):
                    n = 4 * t + i
                    act.wait_ge(aT_done.sem, aT_done.at(m, n + 1))
                    act.wait_ge(o_done.sem, o_done.at(m - 1, t + 1))
                    act.activation(attnT[:, t, 4 * i:4 * i + 4, :],
                                   s_ps[0:NK, n % SB, :].rearrange("p (h n) -> p h n", h=4),
                                   ACT.Copy).then_inc(aT_taken.sem, 1)
                act.wait_ge(o_done.sem, o_done.at(m, t + 1))
                act.wait_ge(wo_done.sem, wo_done.at(m - 1))
                act.activation(OT[:, :, t * P:(t + 1) * P], pair(t), ACT.Copy).then_inc(o_taken.sem, 1)

            def late_turned(m, p):
                act.wait_ge(l1_done.sem, l1_done.at(m - 2))
                for t in range(T):
                    act.wait_ge(x1T_done.sem, x1T_done.at(m, t + 1))
                    act.activation(x1nT[:, p, :, t * P:(t + 1) * P], pair(t), ACT.Copy).then_inc(x1T_taken.sem, 1)

            def late_sigmoids(m):
                act.wait_ge(logits_done.sem, logits_done.at(m))
                act.wait_ge(w_ready.sem, w_ready.at(m - 1))
                act.activation(sigm[:].rearrange("p t e -> p (t e)"), m_ps[:, 0, 0:T * E],
                               ACT.Sigmoid).then_inc(logits_sigm.sem, 1)

            def late_roots(f):
                act.wait_ge(swT_done.sem, swT_done.at(f))
                act.wait_ge(sw_stored.sem, sw_stored.at(f - 1))
                act.activation(swT[:], m_ps[0:E, 1, 0:TOK], ACT.Copy).then_inc(swT_taken.sem, 1)

            def old_shared(f):
                act.wait_ge(l1_done.sem, l1_done.at(f, 1))
                act.activation(g[:, 0], h_ps[:, 0], ACT.Relu).then_inc(gated.sem, 1)

            def old_square(f, i):
                act.wait_ge(gated.sem, gated.at(f, i + 1))
                act.wait_ge(l2_done.sem, l2_done.at(f, i - 1))
                act.activation(hid[:, i % 2], g[:, i % 2], ACT.Square).then_inc(hid_ready.sem, 1)

            def turn(b, p, q, new=False, mid=False, late=False, old=False, ahead=True):
                def square(i):
                    if old and i == 0:
                        old_shared(b - 3)
                    if old:
                        old_square(b - 3, i)

                if new:
                    new_context(b)
                    new_keys(b)
                    new_turned(b, 0)
                square(0)
                if new:
                    new_turned(b, 1)
                    new_queries(b)
                square(1)
                if mid:
                    sign_relu(b - 1, q, 2, 0)
                    sign_relu(b - 1, q, 2, 1)
                if new:
                    new_scores(b, p, 0)
                square(2)
                if new:
                    new_scores(b, p, 1)
                if late:
                    late_product(b - 2, 0)
                square(3)
                if mid:
                    sign_relu(b - 1, q, 3, 0)
                    sign_relu(b - 1, q, 3, 1)
                if late:
                    late_product(b - 2, 1)
                square(4)
                if new:
                    sign_relu(b, p, 0, 0)
                    sign_relu(b, p, 0, 1)
                square(5)
                if late:
                    late_norm(b - 2, p)
                if late:
                    late_turned(b - 2, p)
                if mid:
                    mid_attention(b - 1, 0)
                square(6)
                if late:
                    late_sigmoids(b - 2)
                if mid:
                    mid_attention(b - 1, 1)
                square(7)
                if new and ahead:
                    new_norm(b + 1, q)
                if new:
                    sign_relu(b, p, 1, 0)
                square(8)
                if new:
                    sign_relu(b, p, 1, 1)
                if late:
                    late_roots(b - 2)

            turns(act, turn, lambda: new_norm(0, 0))

        @block.tensor
        def _(pe):
            pe.wait_ge(w_att, 16 * N_ATT_LOADS)
            pe.wait_ge(consts, N_CONSTS)

            def late_roots(f, new):
                pe.wait_ge(sw_ready.sem, sw_ready.at(f))
                pe.wait_ge(x1T_taken.sem, x1T_taken.at(f))
                if new:
                    pe.wait_ge(v_taken.sem, v_taken.at(f + 2))
                for t in range(T):
                    last = pe.transpose(m_ps[0:E, 1, t * P:(t + 1) * P], sw[:, t, :], ident[:])
                last.then_inc(swT_done.sem, 1)

            def new_context(b):
                pe.wait_ge(ctx_loaded.sem, ctx_loaded.at(b))
                pe.wait_ge(gate_chain.sem, gate_chain.at(b - 3, 1))
                for k in range(KC):
                    last = pe.transpose(m_ps[:, 0, k * NK:(k + 1) * NK], ctx_sb[:, k * P:(k + 1) * P],
                                        ident[0:NK, 0:NK])
                last.then_inc(ctxT_done.sem, 1)

            def new_keys(b):
                pe.wait_ge(ctxT_taken.sem, ctxT_taken.at(b))
                pe.wait_ge(v_taken.sem, v_taken.at(b - 1))
                pe.wait_ge(swT_taken.sem, swT_taken.at(b - 3))
                for c in range(KC):
                    for k in range(KC):
                        last = pe.matmul(m_ps[:, 1, c * NK:(c + 1) * NK], wk_sb[:, k, c * P:(c + 1) * P],
                                         ctxT[:, k, :], start=(k == 0), stop=(k == KC - 1))
                last.then_inc(k_done.sem, 1)

            def new_values(b, late):
                pe.wait_ge(q_taken.sem, q_taken.at(b))
                if late:
                    pe.wait_ge(x1T_taken.sem, x1T_taken.at(b - 2))
                for k in range(KC):
                    last = pe.matmul(m_ps[0:NK, 1, 0:D], ctxT[:, k, :], wv_sb[:, k, :],
                                     start=(k == 0), stop=(k == KC - 1))
                last.then_inc(v_done.sem, 1)

            def new_turned(b, t):
                pe.wait_ge(xn_ready.sem, xn_ready.at(b, t + 1))
                if t:
                    pe.wait_ge(k_taken.sem, k_taken.at(b))
                for k in range(KC):
                    last = pe.transpose(m_ps[:, t, k * P:(k + 1) * P], xn[:, t, k * P:(k + 1) * P], ident[:])
                last.then_inc(xT_done.sem, 1)

            def new_queries(b):
                pe.wait_ge(xT_taken.sem, xT_taken.at(b))
                for c in range(KC):
                    for k in range(KC):
                        last = pe.matmul(m_ps[:, c, 0:TOK], wq_sb[:, k, c * P:(c + 1) * P], xnT[:, k, :],
                                         start=(k == 0), stop=(k == KC - 1))
                    last.then_inc(q_done.sem, 1)

            def new_scores(b, t):
                pe.wait_ge(q_taken.sem, q_taken.at(b))
                pe.wait_ge(k_diag_ready.sem, k_diag_ready.at(b))
                if t:
                    pe.wait_ge(s_taken.sem, s_taken.at(b, t))
                else:
                    pe.wait_ge(aT_taken.sem, aT_taken.at(b - 3))
                for c, h0, n, bank, col in ((0, 0, 6, 0, 0), (0, 6, 2, 1, 0), (1, 0, 4, 1, 2), (1, 4, 4, 2, 0)):
                    last = pe.matmul(s_ps[:, bank, col * NK:(col + n) * NK], qT[:, c, t * P:(t + 1) * P],
                                     k_diag[:, c, h0:h0 + n, :].rearrange("p h k -> p (h k)"),
                                     start=True, stop=True)
                last.then_inc(s_done.sem, 1)

            def late_unsettled(m):
                pe.wait_ge(unsettled_known.sem, unsettled_known.at(m))
                pe.wait_ge(y_ready.sem, y_ready.at(m - 2))
                pe.matmul(y_ps[0:1, 0, 0:1], unsettled_any[:], ones[:], start=True, stop=True
                          ).then_inc(count_done.sem, 1)

            def late_product(m, p, t, new):
                pe.wait_ge(attn_checked.sem, attn_checked.at(m))
                if new:
                    pe.wait_ge(s_taken.sem, s_taken.at(m + 2))
                else:
                    pe.wait_ge(gate_chain.sem, gate_chain.at(m - 1, 1))
                for i in range(4):
                    n = 4 * t + i
                    pe.wait_ge(aT_taken.sem, aT_taken.at(m, n - SB + 1))
                    for j in range(4):
                        last = pe.transpose(s_ps[0:NK, n % SB, j * P:(j + 1) * P], attn[:, t, 4 * i + j, :], ident[:])
                    last.then_inc(aT_done.sem, 1)
                for i in range(4):
                    pe.wait_ge(aT_taken.sem, aT_taken.at(m, 4 * t + i + 1))
                    for j in (0, 2, 1, 3):
                        h = 4 * i + j
                        c, quad = h // 8, h % 8 // 2
                        last = pe.matmul(m_ps[32 * quad:32 * quad + 32, t, c * P:(c + 1) * P], v_pad[:, p, h, :],
                                         attnT[:, t, h, :], start=(h % 2 == 0), stop=(h % 2 == 1))
                last.then_inc(o_done.sem, 1)

            def late_output(m):
                for t in range(T):
                    pe.wait_ge(o_taken.sem, o_taken.at(m, t + 1))
                    for c in range(KC):
                        last = pe.matmul(m_ps[:, t, 0:D], OT[:, c, t * P:(t + 1) * P], wo_sb[:, c, :],
                                         start=(c == 0), stop=(c == KC - 1))
                    last.then_inc(wo_done.sem, 1)

            def late_turned(m):
                for t in range(T):
                    pe.wait_ge(x1n_ready.sem, x1n_ready.at(m, t + 1))
                    for k in range(KC):
                        last = pe.transpose(m_ps[:, t, k * P:(k + 1) * P], x1n[:, t, k * P:(k + 1) * P], ident[:])
                    last.then_inc(x1T_done.sem, 1)

            def late_route(m, p):
                pe.wait_ge(w_ffn, 16 * 5)
                pe.wait_ge(x1T_taken.sem, x1T_taken.at(m))
                for t in range(T):
                    for k in range(KC):
                        last = pe.matmul(m_ps[:, 0, t * E:(t + 1) * E], x1nT[:, p, k, t * P:(t + 1) * P],
                                         gate_sb[:, k, :], start=(k == 0), stop=(k == KC - 1))
                last.then_inc(logits_done.sem, 1)

            def layer1(f, p, i):
                e = ORDER[i]
                if i == 0:
                    pe.wait_ge(w_ffn, 16 * 5)
                pe.wait_ge(gated.sem, gated.at(f, i - 1))
                for c in range(KC):
                    for k in range(KC):
                        last = pe.matmul(h_ps[:, i % 2, c, :], w1_sb[:, e, k, c * P:(c + 1) * P], x1nT[:, p, k, :],
                                         start=(k == 0), stop=(k == KC - 1))
                last.then_inc(l1_done.sem, 1)

            def layer2(f, i, late):
                e = ORDER[i]
                pe.wait_ge(hid_ready.sem, hid_ready.at(f, i + 1))
                if i == 0:
                    pe.wait_ge(y_ready.sem, y_ready.at(f - 1))
                    if late:
                        pe.wait_ge(count_taken.sem, count_taken.at(f + 1))
                for t in range(T):
                    for c in range(KC):
                        last = pe.matmul(y_ps[:, t, :], hid[:, i % 2, c, t * P:(t + 1) * P], w2_sb[:, e, c, :],
                                         start=(i == 0 and t == 0 and c == 0),
                                         stop=(i == EXPERTS - 1 and c == KC - 1), skip_group_check=True)
                last.then_inc(l2_done.sem, 1)

            def turn(b, p, q, new=False, mid=False, late=False, old=False, ahead=True):
                def l1(i):
                    if old:
                        layer1(b - 3, q, i)

                def l2(i):
                    if old:
                        layer2(b - 3, i, late)

                if new:
                    new_context(b)
                l1(0)
                if late:
                    late_unsettled(b - 2)
                if new:
                    new_keys(b)
                    new_turned(b, 0)
                l1(1)
                if new:
                    new_turned(b, 1)
                l2(0)
                if new:
                    new_queries(b)
                l1(2)
                if new:
                    new_scores(b, 0)
                l2(1)
                l1(3)
                if new:
                    new_scores(b, 1)
                l2(2)
                if late:
                    late_product(b - 2, p, 0, new)
                l1(4)
                l2(3)
                l1(5)
                if late:
                    late_product(b - 2, p, 1, new)
                if late:
                    late_output(b - 2)
                l2(4)
                l1(6)
                l2(5)
                if late:
                    late_turned(b - 2)
                l1(7)
                if late:
                    late_route(b - 2, p)
                if new:
                    new_values(b, late)
                l2(6)
                l1(8)
                l2(7)
                l2(8)
                if late:
                    late_roots(b - 2, new)

            turns(pe, turn)

        @block.vector
        def _(dve):
            for t, v in ((v_pad, 0.0), (signs[:, :, :, :, NK:SW - 1], 26.0), (signs[:, :, :, :, SW - 1:], 25.0)):
                dve.memset(t[:], v).then_inc(consts, 1)
            dve.wait_ge(w_att, 16 * N_ATT_LOADS)
            dve.wait_ge(consts, N_CONSTS)

            def norm_stats(b, t, src, stats, mv, minus, veps, chain, ready):
                dve.bn_stats(stats[:, t], src).then_inc(chain.sem, 1)
                dve.wait_ge(chain.sem, chain.at(b, 2 * t + 1))
                stand(dve)
                dve.bn_aggr(mv[:, t], stats[:, t]).then_inc(chain.sem, 1)
                dve.wait_ge(chain.sem, chain.at(b, 2 * t + 2))
                dve.tensor_scalar(minus[:, t:t + 1], mv[:, t, 0:1], -1.0, None, ALU.mult)
                dve.tensor_scalar(veps[:, t:t + 1], mv[:, t, 1:2], LN_EPS, None, ALU.add).then_inc(ready.sem, 1)

            def new_stats(b, p):
                dve.wait_ge(x_loaded[p], x_loads(b))
                dve.wait_ge(shift_ready.sem, shift_ready.at(b - 1))
                for t in range(T):
                    norm_stats(b, t, x_sb[:, p, t], ln_stats, ln_mv, ln_minus, ln_veps, ln_chain, veps_ready)

            def new_values(b, p):
                dve.wait_ge(v_done.sem, v_done.at(b))
                dve.wait_ge(o_done.sem, o_done.at(b - 2))
                src = m_ps[0:NK, 1, 0:D].rearrange("p (a j d) -> p a j d", j=2, d=DH)
                bias = bv_sb[:].rearrange("p (a j d) -> p a j d", j=2, d=DH)
                for j in range(2):
                    dst = v_pad[:, p].rearrange("p (a j) d -> p a j d", j=2)[:, :, j, j * DH:(j + 1) * DH]
                    dve.tensor_tensor(dst, src[:, :, j, :], bias[:, :, j, :], ALU.add).then_inc(v_taken.sem, 1)

            def new_tau(b, p, t):
                dve.wait_ge(s_taken.sem, s_taken.at(b, t + 1))
                stand(dve)
                for h in range(NH):
                    last = dve.max(top8[:, t, h], S[:, p, t, h])
                last.then_inc(top_chain.sem, 1)
                dve.wait_ge(top_chain.sem, top_chain.at(b, 3 * t + 1))
                top = top8[:, t].rearrange("p h k -> p (h k)")
                dve.tensor_tensor_scan(csum[:, t], keep[:], top, 0.0, ALU.mult, ALU.add).then_inc(top_chain.sem, 1)
                dve.wait_ge(top_chain.sem, top_chain.at(b, 3 * t + 2))
                dve.scalar_tensor_tensor(bounds[:, t], csum[:, t], -1.0, inv_k[:], ALU.add, ALU.mult
                                         ).then_inc(top_chain.sem, 1)
                dve.wait_ge(top_chain.sem, top_chain.at(b, 3 * t + 3))
                dve.tensor_reduce(tau[:, p, t], bounds[:, t].rearrange("p (h k) -> p h k", k=8), AX.X, ALU.max
                                  ).then_inc(tau_first.sem, 1)

            def newton(b, p, r, between):
                n0 = 4 * r
                for t in range(T):
                    dve.wait_ge(sign_done.sem, sign_done.at(b, rt(r, t)))
                    dve.tensor_tensor(fold_a[:, t], signs[:, p, t, :, 0:SW // 2], signs[:, p, t, :, SW // 2:], ALU.add
                                      ).then_inc(signs_folded.sem, 1)
                    dve.wait_ge(relu_done.sem, relu_done.at(b, rt(r, t)))
                    dve.tensor_reduce(fsum[:, t * NH:(t + 1) * NH], over[:, p, t], AX.X, ALU.add
                                      ).then_inc(f_summed.sem, 1)
                dve.wait_ge(signs_folded.sem, signs_folded.at(b, rt(r, 1)))
                halves = fold_a[:].rearrange("p t h k -> p (t h) k")
                dve.tensor_tensor(fold_b[:], halves[:, :, 0:SW // 4], halves[:, :, SW // 4:], ALU.add
                                  ).then_inc(newton_chain.sem, 1)
                between()
                dve.wait_ge(newton_chain.sem, newton_chain.at(b, n0 + 1))
                dve.tensor_reduce(den[:], fold_b[:], AX.X, ALU.add).then_inc(newton_chain.sem, 1)
                dve.wait_ge(newton_chain.sem, newton_chain.at(b, n0 + 2))
                dve.reciprocal(rden[:], den[:]).then_inc(newton_chain.sem, 1)
                dve.wait_ge(newton_chain.sem, newton_chain.at(b, n0 + 3))
                dve.scalar_tensor_tensor(step[:], fsum[:], -1.0, rden[:], ALU.add, ALU.mult
                                         ).then_inc(newton_chain.sem, 1)
                dve.wait_ge(newton_chain.sem, newton_chain.at(b, n0 + 4))
                dve.scalar_tensor_tensor(flat(tau[:, p]), step[:], 2.0, flat(tau[:, p]), ALU.mult, ALU.add
                                         ).then_inc(tau_ready.sem, 1)

            def flat(ap):
                return ap.rearrange("p t h -> p (t h)")

            def mid_tolerance(m, p):
                tau_m = flat(tau[:, p])
                dve.wait_ge(tau_ready.sem, tau_ready.at(m))
                dve.scalar_tensor_tensor(tol[:], tau_m, -1.0, tau_m, ALU.mult, ALU.max).then_inc(check_chain.sem, 1)
                dve.wait_ge(check_chain.sem, check_chain.at(m, 1))
                dve.tensor_scalar(tol[:], tol[:], 1.0, 5e-7, ALU.max, ALU.mult).then_inc(check_chain.sem, 1)
                dve.wait_ge(check_chain.sem, check_chain.at(m, 2))
                dve.tensor_tensor(tol[:], tol[:], den[:], ALU.mult).then_inc(check_chain.sem, 1)

            def mid_check(m):
                for t in range(T):
                    dve.wait_ge(attn_ready.sem, attn_ready.at(m, t + 1))
                    dve.tensor_reduce(asum[:, t * NH:(t + 1) * NH], attn[:, t], AX.X, ALU.add
                                      ).then_inc(attn_summed.sem, 1)
                dve.wait_ge(check_chain.sem, check_chain.at(m, 3))
                dve.wait_ge(attn_summed.sem, attn_summed.at(m))
                dve.scalar_tensor_tensor(unsettled[:], asum[:], -1.0, tol[:], ALU.add, ALU.is_gt
                                         ).then_inc(check_chain.sem, 1)
                dve.wait_ge(check_chain.sem, check_chain.at(m, 4))
                dve.tensor_reduce(unsettled_any[:], unsettled[:], AX.X, ALU.add).then_inc(unsettled_known.sem, 1)

            def late_verdict(m):
                dve.wait_ge(count_done.sem, count_done.at(m))
                dve.tensor_copy(unsettled_count[:], y_ps[0:1, 0, 0:1]).then_inc(count_taken.sem, 1)

            def late_settle(m, p):
                dve.wait_ge(count_taken.sem, count_taken.at(m))
                stand(dve)
                count = dve.value_load(unsettled_count[0:1, 0:1], min_val=0, max_val=P * T * NH)
                with dve.If(count > 0):
                    spare_steps(p)
                dve.engine_nop().then_inc(attn_checked.sem, 1)

            def spare_steps(p):
                all_s, all_r = (a.rearrange("p t h k -> p (t h) k") for a in (S[:, p], attn[:]))
                tau_m = flat(tau[:, p])
                tau_row = tau_m.rearrange("p (h o) -> p h o", o=1).broadcast_to([P, T * NH, NK])
                K = 9
                with dve.Fori(0, SPARE) as s:
                    dve.tensor_tensor(all_r, all_s, tau_row, ALU.subtract).then_inc(spare_step, 1)
                    dve.wait_ge(spare_step, s * K + 1)
                    dve.tensor_scalar(all_r, all_r, 0.0, None, ALU.max).then_inc(spare_step, 1)
                    dve.wait_ge(spare_step, s * K + 2)
                    dve.tensor_reduce(spare_f[:], all_r, AX.X, ALU.add).then_inc(spare_step, 1)
                    dve.wait_ge(spare_step, s * K + 3)
                    dve.tensor_tensor(all_r, all_s, tau_row, ALU.is_gt).then_inc(spare_step, 1)
                    dve.wait_ge(spare_step, s * K + 4)
                    dve.tensor_reduce(spare_n[:], all_r, AX.X, ALU.add).then_inc(spare_step, 1)
                    dve.wait_ge(spare_step, s * K + 5)
                    dve.tensor_scalar(spare_n[:], spare_n[:], 1.0, None, ALU.max).then_inc(spare_step, 1)
                    dve.wait_ge(spare_step, s * K + 6)
                    dve.reciprocal(spare_r[:], spare_n[:]).then_inc(spare_step, 1)
                    dve.wait_ge(spare_step, s * K + 7)
                    dve.scalar_tensor_tensor(spare_f[:], spare_f[:], -1.0, spare_r[:], ALU.add, ALU.mult
                                             ).then_inc(spare_step, 1)
                    dve.wait_ge(spare_step, s * K + 8)
                    dve.tensor_tensor(tau_m, tau_m, spare_f[:], ALU.add).then_inc(spare_step, 1)
                    dve.wait_ge(spare_step, s * K + 9)
                    stand(dve)
                dve.tensor_tensor(all_r, all_s, tau_row, ALU.subtract).then_inc(spare_step, 1)
                dve.wait_ge(spare_step, SPARE * K + 1)
                dve.tensor_scalar(all_r, all_r, 0.0, None, ALU.max).then_inc(spare_step, 1)
                dve.wait_ge(spare_step, SPARE * K + 2)
                dve.sem_clear(spare_step)

            def late_stats(m, p):
                dve.wait_ge(f_shift_ready.sem, f_shift_ready.at(m - 1))
                dve.wait_ge(xb_ready.sem, xb_ready.at(m))
                for t in range(T):
                    dve.wait_ge(wo_done.sem, wo_done.at(m, t + 1))
                    dve.tensor_tensor(x1[:, p, t], m_ps[:, t, 0:D], xb[:, p, t], ALU.add).then_inc(x1_done.sem, 1)
                for t in range(T):
                    dve.wait_ge(x1_done.sem, x1_done.at(m, t + 1))
                    norm_stats(m, t, x1[:, p, t], f_stats, f_mv, f_minus, f_veps, f_chain, f_veps_ready)

            def late_gate(m):
                dve.wait_ge(logits_sigm.sem, logits_sigm.at(m))
                dve.tensor_tensor(biased[:], m_ps[:, 0, 0:T * E].rearrange("p (t e) -> p t e", t=T),
                                  lb_sb[:].rearrange("p (o e) -> p o e", o=1).broadcast_to([P, T, E]),
                                  ALU.add).then_inc(gate_chain.sem, 1)
                dve.wait_ge(gate_chain.sem, gate_chain.at(m, 1))
                stand(dve)
                for t in range(T):
                    last = dve.max(best[:, t], biased[:, t])
                last.then_inc(gate_chain.sem, 1)
                dve.wait_ge(gate_chain.sem, gate_chain.at(m, 2))
                stand(dve)
                for t in range(T):
                    last = dve.max_index(best_at[:, t], best[:, t], biased[:, t])
                last.then_inc(gate_chain.sem, 1)
                dve.wait_ge(gate_chain.sem, gate_chain.at(m, 3))
                dve.tensor_copy(best_f[:], best_at[:, :, 0:2]).then_inc(gate_chain.sem, 1)
                dve.wait_ge(gate_chain.sem, gate_chain.at(m, 4))
                for t in range(T):
                    last = dve.tensor_scalar(first[:, t], iota[:], best_f[:, t, 0:1], None, ALU.is_equal)
                last.then_inc(gate_chain.sem, 1)
                dve.wait_ge(gate_chain.sem, gate_chain.at(m, 5))
                for t in range(T):
                    last = dve.scalar_tensor_tensor(chosen[:, t], iota[:], best_f[:, t, 1:2], first[:, t],
                                                    ALU.is_equal, ALU.add)
                last.then_inc(gate_chain.sem, 1)
                dve.wait_ge(gate_chain.sem, gate_chain.at(m, 6))
                dve.tensor_tensor(wsel[:], sigm[:], chosen[:], ALU.mult).then_inc(gate_chain.sem, 1)
                dve.wait_ge(gate_chain.sem, gate_chain.at(m, 7))
                dve.tensor_reduce(wsum[:], wsel[:], AX.X, ALU.add).then_inc(gate_chain.sem, 1)
                dve.wait_ge(gate_chain.sem, gate_chain.at(m, 8))
                dve.tensor_scalar(wsum[:], wsum[:], 1e-6, None, ALU.add).then_inc(gate_chain.sem, 1)
                dve.wait_ge(gate_chain.sem, gate_chain.at(m, 9))
                dve.reciprocal(wrec[:], wsum[:]).then_inc(gate_chain.sem, 1)
                dve.wait_ge(gate_chain.sem, gate_chain.at(m, 10))
                dve.wait_ge(sw_ready.sem, sw_ready.at(m - 1))
                dve.tensor_tensor(wnorm[:], wsel[:],
                                  wrec[:].rearrange("p (t o) -> p t o", o=1).broadcast_to([P, T, E]),
                                  ALU.mult).then_inc(w_ready.sem, 1)

            def old_gates(f, p, i):
                e = ORDER[i]
                if i == 1:
                    dve.wait_ge(sw_spread.sem, sw_spread.at(f))
                    dve.wait_ge(gated.sem, gated.at(f, 1))
                dve.wait_ge(l1_done.sem, l1_done.at(f, i + 1))
                dve.wait_ge(hid_ready.sem, hid_ready.at(f, i - 1))
                dve.scalar_tensor_tensor(g[:, i % 2], h_ps[:, i % 2], 0.0,
                                         sw_all[:, p, e:e + 1, :].broadcast_to([P, KC, TOK]),
                                         ALU.max, ALU.mult).then_inc(gated.sem, 1)

            def old_finish(f, p):
                dve.wait_ge(l2_done.sem, l2_done.at(f))
                dve.wait_ge(out_stored.sem, out_stored.at(f - 1))
                for t in range(T):
                    dve.tensor_tensor(y[:, t], y_ps[:, t, :], x1[:, p, t], ALU.add).then_inc(y_ready.sem, 1)

            def turn(b, p, q, new=False, mid=False, late=False, old=False, ahead=True):
                def gates(i):
                    if old:
                        old_gates(b - 3, q, i)

                def newton_and_gates(stage, b, p, r, i):
                    if stage:
                        newton(b, p, r, lambda: gates(i))
                    else:
                        gates(i)

                def verdict():
                    if late:
                        late_verdict(b - 2)

                if mid:
                    newton(b - 1, q, 1, verdict)
                else:
                    verdict()
                gates(1)
                if new and ahead:
                    new_stats(b + 1, q)
                if late:
                    late_settle(b - 2, p)
                newton_and_gates(mid, b - 1, q, 2, 2)
                if new:
                    new_tau(b, p, 0)
                gates(3)
                if new:
                    new_tau(b, p, 1)
                newton_and_gates(mid, b - 1, q, 3, 4)
                if mid:
                    mid_tolerance(b - 1, q)
                if late:
                    late_stats(b - 2, p)
                gates(5)
                newton_and_gates(new, b, p, 0, 6)
                gates(7)
                if late:
                    late_gate(b - 2)
                if new:
                    new_values(b, p)
                gates(8)
                if mid:
                    mid_check(b - 1)
                if old:
                    old_finish(b - 3, q)

            turns(dve, turn, lambda: new_stats(0, 0))


def kernel(**inputs):
    import concourse.bacc as bacc
    from concourse.bass_utils import run_bass_kernel_spmd

    a = {k.replace("L0_xattn_", "").replace("L0_ffn_", ""): np.ascontiguousarray(v) for k, v in inputs.items()}

    def turned(w):
        return np.ascontiguousarray(np.swapaxes(w, -1, -2))

    arrays = {
        "x": a["x"], "ctx": a["ctx_1024"], "wq": a["Wq"], "wk": a["Wk"], "wv": a["Wv"], "wo": a["Wo"],
        "bq": turned(a["bq"].reshape(KC, P)), "bk": turned(a["bk"].reshape(KC, P)), "bv": a["bv"], "bo": a["bo"],
        "gate_w": turned(a["gate_w"]), "lb_bias": a["lb_bias"], "w1": turned(a["w1"]), "w2": turned(a["w2"]),
        "cfc": turned(a["cfc"]), "cproj": turned(a["cproj"]),
        "ident": np.eye(P, dtype=np.float32),
        "head_of": np.repeat(np.eye(8, dtype=np.float32), DH, axis=0),
        "iota": np.tile(np.arange(E, dtype=np.float32), (P, 1)),
        "keep": np.tile(np.array([0] + [1] * 7, np.float32), (P, NH)),
        "inv_k": np.tile((1.0 / np.arange(1, 9)).astype(np.float32), (P, NH)),
    }
    nc = bacc.Bacc("TRN2", target_bir_lowering=False, num_devices=1)
    args = [nc.dram_tensor(f"in_{n}", v.shape, mybir.dt.from_np(v.dtype), kind="ExternalInput").ap()
            for n, v in arrays.items()]
    out = nc.dram_tensor("out_y", a["x"].shape, F32, kind="ExternalOutput").ap()
    xattn_moe_kernel(nc, *args, out)
    r = run_bass_kernel_spmd(nc, [{f"in_{n}": v for n, v in arrays.items()}], core_ids=[0])
    return r.results[0]["out_y"]
```
